# Optimizing a Trainium2 kernel written in Bass

```python
import numpy as np
import jax
import jax.numpy as jnp

def _softmax(x, axis=-1):
    return jax.nn.softmax(x, axis=axis)

def _gelu(x):
    return jax.nn.gelu(x, approximate=True)

def _silu(x):
    return jax.nn.silu(x)

def _sigmoid(x):
    return jax.nn.sigmoid(x)

def _layernorm(x, axis=-1, eps=1e-05):
    m = jnp.mean(x, axis=axis, keepdims=True)
    v = jnp.var(x, axis=axis, keepdims=True)
    return (x - m) / jnp.sqrt(v + eps)

def _scatter_add(tgt, idx, src, axis=0):
    return tgt.at[idx].add(src)

def _segment_sum(src, seg, n):
    return jax.ops.segment_sum(src, seg, n)
kernel_name = 'mk_prb_d1_jaxref_r8_ddfff2'

def setup_inputs(seed: int=0):
    np.random.seed(seed)
    _w = jnp.asarray

    def _L0_attn_setup():
        import jax, jax.numpy as jnp
        import numpy as np
        D_MODEL = 128
        N_HEADS = 16
        HEAD_DIM = D_MODEL // N_HEADS
        ROPE_BASE = 10000.0

        def _rope(q, k):
            S, Dh = (q.shape[1], q.shape[-1])
            inv_freq = 1.0 / ROPE_BASE ** (jnp.arange(0, Dh, 2, dtype=jnp.float32) / Dh)
            t = jnp.arange(S, dtype=jnp.float32)
            freqs = jnp.outer(t, inv_freq)
            emb = jnp.concatenate([freqs, freqs], axis=-1)
            cos = jnp.cos(emb)[None, :, None, :]
            sin = jnp.sin(emb)[None, :, None, :]

            def rotate_half(v):
                v1, v2 = (v[..., :Dh // 2], v[..., Dh // 2:])
                return jnp.concatenate([-v2, v1], axis=-1)
            return (q * cos + rotate_half(q) * sin, k * cos + rotate_half(k) * sin)
        key = jax.random.key(seed)
        ks = jax.random.split(key, 5)
        B, S = (1, 512)
        scale = 1.0 / np.sqrt(D_MODEL)
        x = jax.random.normal(ks[0], (B, S, D_MODEL), dtype=jnp.float32)
        Wq = jax.random.normal(ks[1], (D_MODEL, D_MODEL), dtype=jnp.float32) * scale
        Wk = jax.random.normal(ks[2], (D_MODEL, D_MODEL), dtype=jnp.float32) * scale
        Wv = jax.random.normal(ks[3], (D_MODEL, D_MODEL), dtype=jnp.float32) * scale
        Wo = jax.random.normal(ks[4], (D_MODEL, D_MODEL), dtype=jnp.float32) * scale
        return {'x': x, 'Wq': Wq, 'Wk': Wk, 'Wv': Wv, 'Wo': Wo}
    _L0_attn_in = _L0_attn_setup()

    def _L0_ffn_setup():
        import jax, jax.numpy as jnp
        import numpy as np
        B, N, C, F, E, K = (2, 256, 128, 512, 8, 2)
        key = jax.random.key(seed)
        k = jax.random.split(key, 6)
        xavier1 = float(np.sqrt(6.0 / (C + F)))
        xavier2 = float(np.sqrt(6.0 / (F + C)))
        return {'x': jax.random.normal(k[0], (B, N, C), dtype=jnp.float32), 'router_w': jax.random.normal(k[1], (E, C), dtype=jnp.float32) * 0.01, 'w1': jax.random.uniform(k[2], (E, F, C), dtype=jnp.float32, minval=-xavier1, maxval=xavier1), 'b1': jnp.zeros((E, F), dtype=jnp.float32), 'w2': jax.random.uniform(k[3], (E, C, F), dtype=jnp.float32, minval=-xavier2, maxval=xavier2), 'b2': jnp.zeros((E, C), dtype=jnp.float32)}
    _L0_ffn_in = _L0_ffn_setup()
    _d = {'L0_attn_x': _L0_attn_in['x'], 'L0_attn_Wq': _L0_attn_in['Wq'], 'L0_attn_Wk': _L0_attn_in['Wk'], 'L0_attn_Wv': _L0_attn_in['Wv'], 'L0_attn_Wo': _L0_attn_in['Wo'], 'L0_ffn_router_w': _L0_ffn_in['router_w'], 'L0_ffn_w1': _L0_ffn_in['w1'], 'L0_ffn_b1': _L0_ffn_in['b1'], 'L0_ffn_w2': _L0_ffn_in['w2'], 'L0_ffn_b2': _L0_ffn_in['b2']}
    _x0 = _d['L0_attn_x']
    _d['L0_attn_x'] = jax.random.normal(jax.random.fold_in(jax.random.key(seed), 1), (4, 1024, 128), dtype=_x0.dtype)
    del _x0
    return _d

def reference(L0_attn_x, L0_attn_Wq, L0_attn_Wk, L0_attn_Wv, L0_attn_Wo, L0_ffn_router_w, L0_ffn_w1, L0_ffn_b1, L0_ffn_w2, L0_ffn_b2):

    def _L0_attn_ref(x, Wq, Wk, Wv, Wo):
        import jax, jax.numpy as jnp
        import numpy as np
        D_MODEL = 128
        N_HEADS = 16
        HEAD_DIM = D_MODEL // N_HEADS
        ROPE_BASE = 10000.0

        def _rope(q, k):
            S, Dh = (q.shape[1], q.shape[-1])
            inv_freq = 1.0 / ROPE_BASE ** (jnp.arange(0, Dh, 2, dtype=jnp.float32) / Dh)
            t = jnp.arange(S, dtype=jnp.float32)
            freqs = jnp.outer(t, inv_freq)
            emb = jnp.concatenate([freqs, freqs], axis=-1)
            cos = jnp.cos(emb)[None, :, None, :]
            sin = jnp.sin(emb)[None, :, None, :]

            def rotate_half(v):
                v1, v2 = (v[..., :Dh // 2], v[..., Dh // 2:])
                return jnp.concatenate([-v2, v1], axis=-1)
            return (q * cos + rotate_half(q) * sin, k * cos + rotate_half(k) * sin)
        B, S, _ = x.shape
        H, Dh = (N_HEADS, HEAD_DIM)
        q = (x @ Wq.T).reshape(B, S, H, Dh)
        k = (x @ Wk.T).reshape(B, S, H, Dh)
        v = (x @ Wv.T).reshape(B, S, H, Dh)
        q, k = _rope(q, k)
        scale = 1.0 / np.sqrt(Dh)
        scores = jnp.einsum('bqhd,bkhd->bhqk', q, k) * scale
        causal = jnp.triu(jnp.ones((S, S), dtype=bool), k=1)
        scores = jnp.where(causal, -jnp.inf, scores)
        attn = jax.nn.softmax(scores, axis=-1)
        out = jnp.einsum('bhqk,bkhd->bqhd', attn, v).reshape(B, S, H * Dh)
        return out @ Wo.T

    def _L0_ffn_ref(x, router_w, w1, b1, w2, b2):
        import jax, jax.numpy as jnp
        import numpy as np
        B, N, C, F, E, K = (2, 256, 128, 512, 8, 2)
        Bb, Nn, Cc = x.shape
        x_flat = x.reshape(-1, Cc)
        logits = jnp.einsum('tc,ec->te', x_flat, router_w)
        probs = jax.nn.softmax(logits, axis=-1)
        top_w, top_idx = jax.lax.top_k(probs, K)
        top_w = top_w / (jnp.sum(top_w, axis=-1, keepdims=True) + 1e-09)
        h = jnp.einsum('tc,efc->tef', x_flat, w1) + b1[None]
        h = jax.nn.relu(h)
        y = jnp.einsum('tef,ecf->tec', h, w2) + b2[None]
        sel = jnp.take_along_axis(y, top_idx[:, :, None], axis=1)
        out = jnp.einsum('tkc,tk->tc', sel, top_w)
        return out.reshape(Bb, Nn, Cc)
    x = L0_attn_x
    xn = _layernorm(x, axis=-1)
    x = x + _L0_attn_ref(xn, L0_attn_Wq, L0_attn_Wk, L0_attn_Wv, L0_attn_Wo) + _L0_ffn_ref(xn, L0_ffn_router_w, L0_ffn_w1, L0_ffn_b1, L0_ffn_w2, L0_ffn_b2)
    return x

_drawn_inputs = setup_inputs


def setup_inputs(seed=0):
    import zlib

    import numpy as np

    out = dict(_drawn_inputs(seed))
    spreads = {'L0_ffn_b1': (0.0, 0.1), 'L0_ffn_b2': (0.0, 0.1)}
    factors = {}
    for name, (base, spread) in spreads.items():
        noise = np.random.default_rng([zlib.crc32(name.encode()), seed]).standard_normal(out[name].shape)
        drawn = base * np.exp(spread * noise) if base else spread * noise
        out[name] = jnp.asarray(drawn.astype(out[name].dtype))
    for name, factor in factors.items():
        out[name] = (out[name] * factor).astype(out[name].dtype)
    return out
```

```python
from contextlib import ExitStack

import concourse.bass as bass
from concourse import mybir

F32 = mybir.dt.float32
BF16 = mybir.dt.bfloat16
ACT = mybir.ActivationFunctionType
ALU = mybir.AluOpType
AX_X = mybir.AxisListType.X

P = 128
B, S, C = 4, 1024, 128
T = S // P
NT = B * T
H, DH = 16, 8
HG = 4
G = H // HG
UNITS = B * G
E, F = 8, 512
FC = F // P
HALF = 512
PARTS = 3
KROWS = PARTS * PARTS * DH
KALL = KROWS + 2
SCALE = DH ** -0.5
BIG = 1e30
EPS = 1e-5


class Steps:

    def __init__(self, eng, sem, base=0):
        self.eng, self.sem, self.base, self.n = eng, sem, base, 0

    def done(self, ins):
        ins.then_inc(self.sem, 1)
        self.n += 1

    def settle(self):
        self.eng.wait_ge(self.sem, self.base + self.n)


def past(n):
    return not (isinstance(n, int) and n == 0)


def max_items():
    items = [(0, [0, 1, 2, 3], P), (1, [0, 1, 2, 3], 2 * P)]
    items += [(qb, hs, HALF) for qb in (2, 3) for hs in ([0, 1], [2, 3])]
    items += [(qb, [h], 2 * HALF) for qb in range(4, T) for h in range(HG)]
    return items


def attention_steps():
    return [(c, kb, max(0, kb - 4 * c) * P) for c in range(2) for kb in range(4 * c + 4)]


def block_program(nc, x, wq, wqs, wk, wks, wv, wo, router, w1, b1, w2, b2, cos_t, sin_t, consts, out,
                  parts_d, heads_d):
    ctx = ExitStack()
    with ctx:
        def sb(name, shape, dt=F32):
            return ctx.enter_context(nc.sbuf_tensor(name, shape, dt))

        def psum(name, shape):
            return ctx.enter_context(nc.psum_tensor(name, shape, F32))

        def sem(name):
            return ctx.enter_context(nc.semaphore(name))

        ITEMS, STEPS = max_items(), attention_steps()
        NI, NS = len(ITEMS), len(STEPS)
        MI = NI + 1
        W_END = 8

        x_all = sb("x_all", [P, NT, C])
        xn = sb("xn", [P, T, C])
        xc = sb("xc", [P, T, C])
        sq = sb("sq", [P, T, C])
        xnT = sb("xnT", [P, S])
        xnT_all = sb("xnT_all", [P, B * S])
        tq = sb("tq", [P, S])
        tk = sb("tk", [P, S])
        qr = sb("qr", [P, S])
        kr = sb("kr", [P, S])
        qsplit = sb("qsplit", [P, PARTS, S], BF16)
        ksplit = sb("ksplit", [P, PARTS, S], BF16)
        cos_s = sb("cos_s", [P, S])
        sin_s = sb("sin_s", [P, S])
        w_proj = sb("w_proj", [P, 6, C])
        w_router = sb("w_router", [P, E])
        stat = sb("stat", [P, 4, T])
        v_all = sb("v_all", [P, UNITS, T, HG * DH])
        logits = sb("logits", [P, NT, E])
        r_a = sb("r_a", [P, NT, E])
        r_b = sb("r_b", [P, NT, E])
        one1 = sb("one1", [P, NT, E])
        one2 = sb("one2", [P, NT, E])
        gates = sb("gates", [P, NT, E])
        r_s = sb("r_s", [P, 4, NT])
        const_s = sb("const_s", [P, 2 * P + E])
        ident = const_s[:, 0:P]
        em8 = const_s[:, 2 * P:2 * P + E]
        ident_b = sb("ident_b", [P, P], BF16)
        mask_b = sb("mask_b", [P, P], BF16)
        eps_s = sb("eps_s", [P, 1])
        qstk = [sb(f"qstk{i}", [KALL, HG, S], BF16) for i in range(2)]
        kstk = [sb(f"kstk{i}", [KALL, HG, S], BF16) for i in range(2)]
        probs = [sb(f"probs{i}", [P, HG, HALF]) for i in range(3)]
        vst = [sb(f"vst{i}", [P, T, HG, 32]) for i in range(2)]
        oraw = [sb(f"oraw{i}", [P, HALF]) for i in range(2)]
        mx = [sb(f"mx{i}", [P, HG, T]) for i in range(2)]
        mneg = [sb(f"mneg{i}", [P, P], BF16) for i in range(2)]
        mrow = [sb(f"mrow{i}", [2 * HG * T, P], BF16) for i in range(2)]
        w1_s = [sb(f"w1_s{i}", [P, F]) for i in range(2)]
        w2_s = [sb(f"w2_s{i}", [P, FC, C]) for i in range(2)]
        b1_s = sb("b1_s", [P, E, FC])
        hid = sb("hid", [P, FC, HALF])
        b2_blk = sb("b2_blk", [P, NT // 2, C])
        gT = sb("gT", [P, 2, P])

        bank = ctx.enter_context(nc.psum_tensor("bank", [P, 8, HALF], F32))
        pair = [bank[:, 2 * i:2 * i + 2, :].rearrange("p a b -> p (a b)") for i in range(4)]
        st = [bank[:, i, :] for i in range(3)]
        pv = bank[:, 3, :]
        ms = [pair[2], pair[3]]

        names = """x_loaded w_loaded tab_loaded const_loaded ln_step ln_centered ln_squared ln_varsum ln_std xn_ready
        xnT_made xnT_ready q_made qs_made k_made ks_made v_made logits_made v_copied logits_copied
        roped q_first q_rest k_first k_rest q_split k_split q_used qs_used k_used ks_used scratch_written
        consts_ready pool_step rt_step rt_shifted rt_exped gates_ready ones_ready
        scores_made scores_read mneg_ready
        diag_seen scoresT_made probs_made diag_masked probs_used heads_copied v_staged
        ffn_b_loaded hid_made hid_ready y_made y_added gT_made gT_copied
        rec_ready att_ready proj_made out_ready out_stored xnT_kept""".split()
        s = {n: sem(n) for n in names}
        mrow_stored = [sem(f"mrow_stored{i}") for i in range(2)]
        stack_loaded = [sem(f"stack_loaded{i}") for i in range(2)]
        heads_stored = [sem(f"heads_stored{i}") for i in range(2)]
        w1_loaded = [sem(f"w1_loaded{i}") for i in range(2)]
        heads_loaded = [sem(f"heads_loaded{i}") for i in range(2)]

        block = ctx.enter_context(nc.Block())
        LN = 3

        def st_of(n):
            return st[n % 3]

        def item_slots(j):
            lo, hi = j * NI // W_END, (j + 1) * NI // W_END
            return range(lo, hi) if j < W_END else ()

        @block.sync
        def _(sp):
            sp.dma_start(const_s[:], consts).then_inc(s["const_loaded"], 16)
            sp.dma_start(x_all[:, 0:T, :], x[0:S, :].rearrange("(t p) c -> p t c", p=P)).then_inc(s["x_loaded"], 16)
            for n, w in enumerate((wq, wqs, wk, wks, wv, wo)):
                sp.dma_start(w_proj[:, n, :], w).then_inc(s["w_loaded"], 16)
            sp.dma_start(w_router[:], router).then_inc(s["w_loaded"], 16)
            for tab, src in ((cos_s, cos_t), (sin_s, sin_t)):
                for h in range(H):
                    sp.dma_start(tab[h * DH:(h + 1) * DH, :], src).then_inc(s["tab_loaded"], 16)
            sp.wait_ge(s["x_loaded"], 16)
            for b in range(1, B):
                sp.dma_start(x_all[:, b * T:(b + 1) * T, :],
                             x[b * S:(b + 1) * S, :].rearrange("(t p) c -> p t c", p=P)).then_inc(s["x_loaded"], 16)
                sp.wait_ge(s["x_loaded"], 16 * (b + 1))
            sp.dma_start(b1_s[:], b1).then_inc(s["ffn_b_loaded"], 16)
            sp.wait_ge(s["ones_ready"], 1)
            for t in range(NT // 2):
                sp.dma_start(b2_blk[t * E:(t + 1) * E, t, :], b2).then_inc(s["ffn_b_loaded"], 16)

            def sequence(b):
                for n, (ready, tile) in enumerate(((s["q_split"], qsplit), (s["k_split"], ksplit))):
                    sp.wait_ge(ready, b + 1)
                    sp.dma_start(parts_d[n, :, bass.ds(b * G, G), :, :].rearrange("a g r s -> (g r) a s"),
                                 tile[:]).then_inc(s["scratch_written"], 16)

            sequence(0)
            with sp.Fori(1, B) as b:
                sequence(b)
            sp.wait_ge(s["scratch_written"], 32 * B)

            def load_stacks(u, par):
                for a in range(PARTS):
                    for r in range(PARTS):
                        at = (a * PARTS + r) * DH
                        for n, stk, part in ((0, qstk[par], a), (1, kstk[par], r)):
                            src = parts_d[n, part, bass.ds(u, 1), :, :]
                            sp.dma_start(stk[at:at + DH, :, :], src.rearrange("o (h d) s -> (o d) h s", d=DH)
                                         ).then_inc(stack_loaded[par], 16)

            def store_max_rows(u, par):
                sp.wait_ge(s["scores_read"], (u + 1) * MI)
                for n in range(2):
                    sp.dma_start(qstk[par][KROWS + n:KROWS + n + 1, :, :].rearrange("o h (t q) -> o (h t) q", q=P),
                                 mrow[par][n * HG * T:(n + 1) * HG * T, :]).then_inc(mrow_stored[par], 16)

            def store_heads(u, c):
                sp.wait_ge(s["heads_copied"], 2 * u + c + 1)
                for h in range(HG):
                    sp.dma_start(heads_d[bass.ds(u, 1), h, :, c * HALF:(c + 1) * HALF].rearrange("u r q -> (u r) q"),
                                 oraw[c][32 * h:32 * h + DH + 1, :]).then_inc(heads_stored[c], 16)

            def unit(i, j, last=False):
                u = 2 * i + j
                nxt = (1 - j)
                if not last:
                    if past(u):
                        sp.wait_ge(s["scoresT_made"], u * (NS * HG))
                    load_stacks(u + 1, nxt)
                store_heads(u, 0)
                if not last:
                    store_max_rows(u + 1, nxt)
                store_heads(u, 1)

            def load_expert(e):
                sp.dma_start(w1_s[e % 2][:], w1[e]).then_inc(w1_loaded[e % 2], 16)
                sp.dma_start(w2_s[e % 2][:], w2[e]).then_inc(w1_loaded[e % 2], 16)

            load_expert(0)
            load_expert(1)
            load_stacks(0, 0)
            store_max_rows(0, 0)
            unit(0, 0)
            unit(0, 1)
            with sp.Fori(1, UNITS // 2 - 1) as i:
                unit(i, 0)
                unit(i, 1)
            unit(UNITS // 2 - 1, 0)
            unit(UNITS // 2 - 1, 1, last=True)

            for e in range(2, E):
                sp.wait_ge(s["y_made"], B * 2 * (e - 1))
                load_expert(e)

            for b in range(B):
                o, d = (xc, sq)[b % 2], (xn, hid)[b % 2]
                for c in range(2):
                    if b == 0:
                        sp.wait_ge(heads_stored[c], 64 * UNITS)
                if b >= 2:
                    sp.wait_ge(s["proj_made"], b - 1)
                if b == 1:
                    sp.wait_ge(s["y_made"], 2 * B * E)
                for h in range(H):
                    u = b * G + h // HG
                    sp.dma_start(o[h * DH:(h + 1) * DH, :, :].rearrange("p t c -> p (t c)"),
                                 heads_d[u, h % HG, 0:DH, :]).then_inc(heads_loaded[b % 2], 16)
                    dv = d[:, :, :].rearrange("p t c -> p (t c)")
                    sp.dma_start(dv[h * DH:(h + 1) * DH, 0:S],
                                 heads_d[u, h % HG, DH:DH + 1, :].broadcast_to([DH, S])
                                 ).then_inc(heads_loaded[b % 2], 16)
            for b in range(B):
                sp.wait_ge(s["out_ready"], b + 1)
                sp.dma_start(out[b * S:(b + 1) * S, :].rearrange("(t p) c -> p t c", p=P),
                             x_all[:, b * T:(b + 1) * T, :]).then_inc(s["out_stored"], 16)
            sp.wait_ge(s["out_stored"], 16 * B)

        @block.gpsimd
        def _(pool):
            k = Steps(pool, s["pool_step"])
            for i in range(2):
                k.done(pool.memset(kstk[i][64:KALL, :, :], 1.0))
                k.settle()
            k.done(pool.memset(b2_blk[:], 0.0))
            k.settle()
            pool.sem_inc(s["ones_ready"], 1)
            for i in range(2):
                k.done(pool.memset(mneg[i][:], 0.0))
                k.settle()
                k.done(pool.memset(vst[i][:], 0.0))
                k.settle()
                k.done(pool.memset(vst[i][:, :, :, DH:DH + 1], 1.0))
                k.settle()
            k.done(pool.memset(eps_s[:], EPS))
            k.settle()
            pool.wait_ge(s["const_loaded"], 16)
            k.done(pool.tensor_copy(ident_b[:], const_s[:, 0:P]))
            k.settle()
            k.done(pool.tensor_copy(mask_b[:], const_s[:, P:2 * P]))
            k.settle()
            pool.sem_inc(s["consts_ready"], 1)
            def sequence(b):
                pool.wait_ge(s["xnT_ready"], b + 1)
                pool.tensor_copy(xnT_all[:, bass.ds(b * S, S)], xnT[:]).then_inc(s["xnT_kept"], 1)

            sequence(0)
            with pool.Fori(1, B) as b:
                sequence(b)

            def stage_v(u, par):
                pool.tensor_copy(vst[par][:, :, :, 0:DH],
                                 v_all[:, bass.ds(u, 1), :, :].rearrange("p o t (h d) -> p (o t) h d", d=DH)
                                 ).then_inc(s["v_staged"], 1)

            def unit(u, par, first, last):
                if not last:
                    if not first:
                        pool.wait_ge(s["probs_used"], u * NS)
                    stage_v(u + 1, 1 - par)
                for n, (c, kb, q0) in enumerate(STEPS):
                    if kb >= 4 * c:
                        pool.wait_ge(s["probs_made"], (u * NS + n + 1) * HG)
                        pool.sem_inc(s["diag_seen"], 1)
                        t = probs[n % 3][:, :, q0:q0 + P]
                        pool.affine_select(out=t, in_=t, compare_op=ALU.is_ge, fill=0.0, base=0,
                                           pattern=[[0, HG], [1, P]], channel_multiplier=-1
                                           ).then_inc(s["diag_masked"], 1)

            pool.wait_ge(s["v_copied"], B)
            stage_v(0, 0)
            unit(0, 0, True, False)
            unit(1, 1, False, False)
            with pool.Fori(1, UNITS // 2 - 1) as i:
                unit(2 * i, 0, False, False)
                unit(2 * i + 1, 1, False, False)
            unit(UNITS - 2, 0, False, False)
            unit(UNITS - 1, 1, False, True)

        @block.scalar
        def _(act):
            act.wait_ge(s["consts_ready"], 1)
            def sequence(b):
                act.wait_ge(s["ln_centered"], b + 1)
                nc.scalar.activation(sq[:], xc[:], ACT.Square).then_inc(s["ln_squared"], 1)
                act.wait_ge(s["ln_varsum"], b + 1)
                nc.scalar.activation(stat[:, 2, :], stat[:, 1, :], ACT.Sqrt, bias=eps_s[:], scale=1.0 / C
                                     ).then_inc(s["ln_std"], 1)
                act.wait_ge(s["xnT_made"], b + 1)
                if past(b):
                    act.wait_ge(s["logits_made"], b)
                    act.wait_ge(s["xnT_kept"], b)
                nc.scalar.copy(xnT[:], pair[0]).then_inc(s["xnT_ready"], 1)
                if past(b):
                    act.wait_ge(s["scratch_written"], 32 * b)
                act.wait_ge(s["roped"], 2 * b + 1)
                nc.scalar.copy(qsplit[:, 0, :], qr[:]).then_inc(s["q_first"], 1)
                act.wait_ge(s["roped"], 2 * b + 2)
                nc.scalar.copy(ksplit[:, 0, :], kr[:]).then_inc(s["k_first"], 1)
                act.wait_ge(s["v_made"], b + 1)
                nc.scalar.copy(v_all[:, bass.ds(b * G, G), :, :].rearrange("p g t e -> p t g e"),
                               pair[1].rearrange("p (t g e) -> p t g e", t=T, g=G)).then_inc(s["v_copied"], 1)
                act.wait_ge(s["q_rest"], b + 1)
                nc.scalar.copy(qsplit[:, 1, :], qr[:]).then_inc(s["q_first"], 1)
                act.wait_ge(s["k_rest"], b + 1)
                nc.scalar.copy(ksplit[:, 1, :], kr[:]).then_inc(s["k_first"], 1)
                act.wait_ge(s["logits_made"], b + 1)
                nc.scalar.copy(logits[:, bass.ds(b * T, T), :],
                               pair[2][:, 0:T * E].rearrange("p (t e) -> p t e", e=E)).then_inc(s["logits_copied"], 1)

            sequence(0)
            with act.Fori(1, B) as b:
                sequence(b)
            act.wait_ge(s["rt_shifted"], 1)
            nc.scalar.activation(r_b[:], r_a[:], ACT.Exp).then_inc(s["rt_exped"], 1)

            def unit(u, lead):
                for n, (c, kb, q0) in enumerate(STEPS):
                    if n >= 3 or not lead:
                        act.wait_ge(s["probs_used"], u * NS + n - 2)
                    for h in range(HG):
                        at = n * HG + h
                        act.wait_ge(s["scoresT_made"], u * (NS * HG) + at + 1)
                        nc.scalar.activation(probs[n % 3][:, h, q0:HALF], st_of(at)[:, 0:HALF - q0], ACT.Exp,
                                             scale=SCALE).then_inc(s["probs_made"], 1)

            unit(0, True)
            with act.Fori(1, UNITS) as u:
                unit(u, False)

            for e in range(E):
                if e == 0:
                    act.wait_ge(s["ffn_b_loaded"], 16 * (1 + NT // 2))
                def chunk(i, e=e):
                    n = e * (NT // 4) + i
                    if past(n):
                        act.wait_ge(s["y_made"], n)
                    for f in range(FC):
                        act.wait_ge(s["hid_made"], n * FC + f + 1)
                        nc.scalar.activation(hid[:, f, :], bank[:, f, :], ACT.Relu, bias=b1_s[:, e, f:f + 1]
                                             ).then_inc(s["hid_ready"], 1)

                if e == 0:
                    chunk(0)
                with act.Fori(int(e == 0), NT // 4) as i:
                    chunk(i)

        @block.vector
        def _(dve):
            v = nc.vector
            dve.wait_ge(s["tab_loaded"], 16 * 2 * H)
            def sequence(b):
                k = Steps(dve, s["ln_step"], b * LN)
                xb = x_all[:, bass.ds(b * T, T), :]
                dve.wait_ge(s["x_loaded"], 16 * (b + 1))
                if past(b):
                    k.settle()
                k.done(v.reduce_sum(stat[:, 0, :], xb, AX_X))
                k.settle()
                k.done(v.tensor_scalar(stat[:, 3, :], stat[:, 0, :], 1.0 / C, None, ALU.mult))
                k.settle()
                v.tensor_tensor(xc[:], xb, stat[:, 3, :].unsqueeze(2).broadcast_to([P, T, C]), ALU.subtract
                                ).then_inc(s["ln_centered"], 1)
                dve.wait_ge(s["ln_squared"], b + 1)
                v.reduce_sum(stat[:, 1, :], sq[:], AX_X).then_inc(s["ln_varsum"], 1)
                dve.wait_ge(s["ln_std"], b + 1)
                k.done(v.reciprocal(stat[:, 3, :], stat[:, 2, :]))
                k.settle()
                dve.wait_ge(s["ln_centered"], b + 1)
                if past(b):
                    dve.wait_ge(s["xnT_made"], b)
                v.tensor_tensor(xn[:], xc[:], stat[:, 3, :].unsqueeze(2).broadcast_to([P, T, C]), ALU.mult
                                ).then_inc(s["xn_ready"], 1)
                for made, mades, used, useds, ps, pss, t, r in (
                        ("q_made", "qs_made", "q_used", "qs_used", pair[1], pair[2], tq, qr),
                        ("k_made", "ks_made", "k_used", "ks_used", pair[3], pair[0], tk, kr)):
                    dve.wait_ge(s[made], b + 1)
                    if past(b):
                        dve.wait_ge(s["q_split" if t is tq else "k_split"], b)
                    v.tensor_tensor(t[:], ps, cos_s[:], ALU.mult).then_inc(s[used], 1)
                    dve.wait_ge(s[mades], b + 1)
                    v.tensor_tensor(r[:], pss, sin_s[:], ALU.mult).then_inc(s[useds], 1)
                    dve.wait_ge(s[used], b + 1)
                    dve.wait_ge(s[useds], b + 1)
                    v.tensor_tensor(r[:], r[:], t[:], ALU.add).then_inc(s["roped"], 1)
                for first, rest, split, r, parts, n in (("q_first", "q_rest", "q_split", qr, qsplit, 1),
                                                        ("k_first", "k_rest", "k_split", kr, ksplit, 2)):
                    dve.wait_ge(s["roped"], 2 * b + n)
                    dve.wait_ge(s[first], 2 * b + 1)
                    v.tensor_tensor(r[:], r[:], parts[:, 0, :], ALU.subtract).then_inc(s[rest], 1)
                for first, rest, split, r, parts in (("q_first", "q_rest", "q_split", qr, qsplit),
                                                     ("k_first", "k_rest", "k_split", kr, ksplit)):
                    dve.wait_ge(s[first], 2 * b + 2)
                    dve.wait_ge(s[rest], b + 1)
                    v.tensor_tensor(parts[:, 2, :], r[:], parts[:, 1, :], ALU.subtract).then_inc(s[split], 1)
                assert k.n == LN

            sequence(0)
            with dve.Fori(1, B) as b:
                sequence(b)

            k = Steps(dve, s["rt_step"])

            def wide(col):
                return r_s[:, col, :].unsqueeze(2).broadcast_to([P, NT, E])

            em = em8.unsqueeze(1).broadcast_to([P, NT, E])
            dve.wait_ge(s["logits_copied"], B)
            k.done(v.reduce_max(r_s[:, 0, :], logits[:], AX_X))
            k.settle()
            v.tensor_tensor(r_a[:], logits[:], wide(0), ALU.subtract).then_inc(s["rt_shifted"], 1)
            dve.wait_ge(s["rt_exped"], 1)
            k.done(v.reduce_sum(r_s[:, 1, :], r_b[:], AX_X))
            k.settle()
            k.done(v.reciprocal(r_s[:, 0, :], r_s[:, 1, :]))
            k.settle()
            k.done(v.tensor_tensor(r_b[:], r_b[:], wide(0), ALU.mult))
            for col, one in ((2, one1), (3, one2)):
                k.settle()
                k.done(v.reduce_max(r_s[:, col, :], r_b[:], AX_X))
                k.settle()
                k.done(v.tensor_tensor(r_a[:], r_b[:], wide(col), ALU.is_equal))
                k.settle()
                k.done(v.tensor_tensor(r_a[:], r_a[:], em, ALU.mult))
                k.settle()
                k.done(v.tensor_reduce(r_s[:, 1, :], r_a[:], AX_X, ALU.min))
                k.settle()
                k.done(v.tensor_tensor(one[:], em, wide(1), ALU.is_equal))
                if col == 2:
                    k.settle()
                    k.done(v.scalar_tensor_tensor(r_b[:], one[:], -2.0, r_b[:], ALU.mult, ALU.add))
            k.settle()
            k.done(v.scalar_tensor_tensor(r_s[:, 0, :], r_s[:, 2, :], 1e-9, r_s[:, 3, :], ALU.add, ALU.add))
            k.settle()
            k.done(v.reciprocal(r_s[:, 1, :], r_s[:, 0, :]))
            for col in (2, 3):
                k.settle()
                k.done(v.tensor_tensor(r_s[:, col, :], r_s[:, col, :], r_s[:, 1, :], ALU.mult))
            k.settle()
            k.done(v.tensor_tensor(gates[:], one1[:], wide(2), ALU.mult))
            k.done(v.tensor_tensor(r_b[:], one2[:], wide(3), ALU.mult))
            k.settle()
            v.tensor_tensor(gates[:], gates[:], r_b[:], ALU.add).then_inc(s["gates_ready"], 1)

            dve.wait_ge(s["consts_ready"], 1)
            def read_item(u, par, n):
                qb, hs, step = ITEMS[n]
                w = (qb + 1) * P
                at = ms[(par * MI + n) % 2]
                dve.wait_ge(s["scores_made"], u * MI + n + 1)
                src = at[:, 0:w] if len(hs) == 1 else at[:, 0:len(hs) * step].rearrange(
                    "p (h w) -> p h w", w=step)[:, :, 0:w]
                v.reduce_max(mx[par][:, hs[0]:hs[-1] + 1, qb], src, AX_X).then_inc(s["scores_read"], 1)

            def split_max(u, par):
                dve.wait_ge(s["scores_read"], u * MI + NI)
                m = mx[par][:].rearrange("p h t -> p (h t)")
                w = HG * T
                v.tensor_scalar(mneg[par][:, 0:w], m, -1.0, None, ALU.mult).then_inc(s["mneg_ready"], 1)
                dve.wait_ge(s["mneg_ready"], 2 * u + 1)
                v.scalar_tensor_tensor(mneg[par][:, w:2 * w], m, -1.0, mneg[par][:, 0:w], ALU.mult, ALU.subtract
                                       ).then_inc(s["mneg_ready"], 1)

            def copy_rows(u, par, seen):
                dve.wait_ge(s["scores_made"], u * MI + MI)
                if seen:
                    dve.wait_ge(mrow_stored[par], 16 * u if par == 0 else 16 * (u - 1))
                src = ms[(par * MI + NI) % 2][0:2 * HG * T, 0:P // 2].bitcast(BF16)
                dve.wait_ge(s["mneg_ready"], 2 * u + 2)
                v.tensor_copy(mrow[par][:], src).then_inc(s["scores_read"], 1)

            def heads_out(u, c, first):
                dve.wait_ge(s["probs_used"], u * NS + (4, NS)[c])
                if not first:
                    dve.wait_ge(heads_stored[c], 64 * u)
                v.tensor_copy(oraw[c][:], pv).then_inc(s["heads_copied"], 1)

            def unit(u, par, first, last):
                for j in range(NS):
                    if not last:
                        for n in item_slots(j):
                            read_item(u + 1, 1 - par, n)
                        if j == W_END - 1:
                            split_max(u + 1, 1 - par)
                        if j == W_END:
                            copy_rows(u + 1, 1 - par, not (first and par == 0))
                    if j == 3:
                        heads_out(u, 0, first and par == 0)
                    if j == NS - 1:
                        heads_out(u, 1, first and par == 0)

            for n in range(NI):
                read_item(0, 0, n)
            split_max(0, 0)
            copy_rows(0, 0, False)
            unit(0, 0, True, False)
            unit(1, 1, True, False)
            with dve.Fori(1, UNITS // 2 - 1) as i:
                unit(2 * i, 0, False, False)
                unit(2 * i + 1, 1, False, False)
            unit(UNITS - 2, 0, False, False)
            unit(UNITS - 1, 1, False, True)

            for e in range(E):
                def chunk(i, e=e):
                    n = e * (NT // 4) + i
                    dve.wait_ge(s["y_made"], n + 1)
                    if past(n):
                        dve.wait_ge(s["y_added"], n * 4)
                    for t in range(4):
                        xt = x_all[:, bass.ds(i * 4 + t, 1), :].rearrange("p o c -> p (o c)")
                        v.scalar_tensor_tensor(xt, bank[:, 4, t * C:(t + 1) * C],
                                               gates[:, bass.ds(i * 4 + t, 1), e], xt, ALU.mult, ALU.add
                                               ).then_inc(s["y_added"], 1)

                if e == 0:
                    chunk(0)
                with dve.Fori(int(e == 0), NT // 4) as i:
                    chunk(i)
            dve.wait_ge(s["gT_made"], 1)
            v.tensor_copy(gT[:].rearrange("p a b -> p (a b)"), bank[:, 5, 0:2 * P]).then_inc(s["gT_copied"], 1)
            for b in range(B):
                o, d = (xc, sq)[b % 2], (xn, hid)[b % 2]
                o2 = o[:].rearrange("p t c -> p (t c)")
                d2 = d[:].rearrange("p t c -> p (t c)")[:, 0:S]
                dve.wait_ge(heads_loaded[b % 2], 16 * 2 * H * (b // 2 + 1))
                v.reciprocal(d2, d2).then_inc(s["rec_ready"], 1)
                dve.wait_ge(s["rec_ready"], b + 1)
                v.tensor_tensor(o2, o2, d2, ALU.mult).then_inc(s["att_ready"], 1)
                dve.wait_ge(s["proj_made"], b + 1)
                if b == 0:
                    dve.wait_ge(s["y_added"], NT * E)
                xt = x_all[:, b * T:(b + 1) * T, :].rearrange("p t c -> p (t c)")
                v.tensor_tensor(xt, pair[b % 2], xt, ALU.add).then_inc(s["out_ready"], 1)

        @block.tensor
        def _(pe):
            mm = nc.tensor.matmul
            pe.wait_ge(s["const_loaded"], 16)
            pe.wait_ge(s["w_loaded"], 16 * 7)
            def sequence(b):
                pe.wait_ge(s["xn_ready"], b + 1)
                if past(b):
                    pe.wait_ge(s["ks_used"], b)
                for t in range(T):
                    last = nc.tensor.transpose(pair[0][:, t * P:(t + 1) * P], xn[:, t, :], ident)
                last.then_inc(s["xnT_made"], 1)
                pe.wait_ge(s["xnT_ready"], b + 1)
                for w, ps, made, free in ((0, 1, "q_made", "v_copied"), (1, 2, "qs_made", "logits_copied"),
                                          (2, 3, "k_made", "k_used"), (3, 0, "ks_made", None)):
                    if free and past(b):
                        pe.wait_ge(s[free], b)
                    for c in range(2):
                        last = mm(pair[ps][:, c * HALF:(c + 1) * HALF], w_proj[:, w, :],
                                  xnT[:, c * HALF:(c + 1) * HALF], start=True, stop=True)
                    last.then_inc(s[made], 1)
                pe.wait_ge(s["q_used"], b + 1)
                for t in range(T):
                    last = mm(pair[1][:, t * C:(t + 1) * C], xnT[:, t * P:(t + 1) * P], w_proj[:, 4, :],
                              start=True, stop=True)
                last.then_inc(s["v_made"], 1)
                pe.wait_ge(s["qs_used"], b + 1)
                for t in range(T):
                    last = mm(pair[2][:, t * E:(t + 1) * E], xnT[:, t * P:(t + 1) * P], w_router[:],
                              start=True, stop=True)
                last.then_inc(s["logits_made"], 1)

            sequence(0)
            with pe.Fori(1, B) as b:
                sequence(b)

            def score_item(u, par, n):
                qb, hs, step = ITEMS[n]
                w = (qb + 1) * P
                at = ms[(par * MI + n) % 2]
                if not (isinstance(u, int) and u * MI + n < 2):
                    pe.wait_ge(s["scores_read"], u * MI + n - 1)
                for i, h in enumerate(hs):
                    lhsT = qstk[par][0:KROWS, h, qb * P:(qb + 1) * P]
                    for k0 in range(0, w, HALF):
                        k1 = min(w, k0 + HALF)
                        mm(at[:, i * step + k0:i * step + k1], lhsT, kstk[par][0:KROWS, h, k0:k1],
                           start=True, stop=k1 < w)
                    last = mm(at[:, i * step + qb * P:i * step + w], ident_b[:], mask_b[:], start=False, stop=True)
                last.then_inc(s["scores_made"], 1)

            def turn_max(u, par):
                pe.wait_ge(s["mneg_ready"], 2 * u + 2)
                pe.wait_ge(s["scores_read"], u * MI + NI - 1)
                nc.tensor.transpose(ms[(par * MI + NI) % 2][:, 0:P // 2].bitcast(BF16), mneg[par][:],
                                    ident_b[:]).then_inc(s["scores_made"], 1)

            def scores(u, par, n, first):
                c, kb, q0 = STEPS[n]
                for h in range(HG):
                    at = n * HG + h
                    if not (first and at < 3):
                        pe.wait_ge(s["probs_made"], u * (NS * HG) + at - 2)
                    mm(st_of(at)[:, 0:HALF - q0], kstk[par][:, h, kb * P:(kb + 1) * P],
                       qstk[par][:, h, c * HALF + q0:(c + 1) * HALF], start=True, stop=True
                       ).then_inc(s["scoresT_made"], 1)

            def products(u, par, n, first):
                c, kb, q0 = STEPS[n]
                if n == 0:
                    pe.wait_ge(s["v_staged"], u + 1)
                if kb == 0 and not (first and c == 0):
                    pe.wait_ge(s["heads_copied"], 2 * u + c)
                pe.wait_ge(s["probs_made"], u * (NS * HG) + (n + 1) * HG)
                if kb >= 4 * c:
                    pe.wait_ge(s["diag_masked"], u * 8 + c * 4 + (kb - 4 * c) + 1)
                for h in range(HG):
                    last = mm(pv[32 * h:32 * h + 32, q0:HALF], vst[par][:, kb, h, :], probs[n % 3][:, h, q0:HALF],
                              start=kb == 0, stop=kb == 4 * c + 3)
                last.then_inc(s["probs_used"], 1)
                if kb == 4 * c + 3:
                    return True

            LEAD = 2

            def unit(u, par, first, last):
                for j in range(NS):
                    if j < NS - LEAD:
                        scores(u, par, j + LEAD, False)
                    elif not last:
                        if j == NS - LEAD:
                            pe.wait_ge(mrow_stored[1 - par], mrow_count(u + 1, 1 - par))
                        scores(u + 1, 1 - par, j + LEAD - NS, False)
                    if not last:
                        if j == 0:
                            pe.wait_ge(stack_loaded[1 - par], stack_count(u + 1, 1 - par))
                        for n in item_slots(j):
                            score_item(u + 1, 1 - par, n)
                        if j == W_END:
                            turn_max(u + 1, 1 - par)
                    products(u, par, j, first)

            def mrow_count(u, par):
                return 16 * (u + 2) if par == 0 else 16 * (u + 1)

            def stack_count(u, par):
                n = 16 * 2 * PARTS * PARTS // 2
                return n * (u + 2) if par == 0 else n * (u + 1)

            pe.wait_ge(s["v_copied"], B)
            pe.wait_ge(s["logits_copied"], B)
            pe.wait_ge(s["k_used"], B)
            pe.wait_ge(s["ks_used"], B)
            pe.wait_ge(s["consts_ready"], 1)
            pe.wait_ge(stack_loaded[0], stack_count(0, 0))
            for n in range(NI):
                score_item(0, 0, n)
            turn_max(0, 0)
            pe.wait_ge(mrow_stored[0], mrow_count(0, 0))
            for n in range(LEAD):
                scores(0, 0, n, True)
            unit(0, 0, True, False)
            unit(1, 1, False, False)
            with pe.Fori(1, UNITS // 2 - 1) as i:
                unit(2 * i, 0, False, False)
                unit(2 * i + 1, 1, False, False)
            unit(UNITS - 2, 0, False, False)
            unit(UNITS - 1, 1, False, True)

            pe.wait_ge(s["heads_copied"], 2 * UNITS)
            for e in range(E):
                pe.wait_ge(w1_loaded[e % 2], 32 * (e // 2 + 1))
                def chunk(i, e=e):
                    n = e * (NT // 4) + i
                    for f in range(FC):
                        mm(bank[:, f, :], w1_s[e % 2][:, f * P:(f + 1) * P], xnT_all[:, bass.ds(i * HALF, HALF)],
                           start=True, stop=True).then_inc(s["hid_made"], 1)
                    pe.wait_ge(s["hid_ready"], (n + 1) * FC)
                    if past(n):
                        pe.wait_ge(s["y_added"], n * 4)
                    for t in range(4):
                        for f in range(FC):
                            last = mm(bank[:, 4, t * C:(t + 1) * C], hid[:, f, t * P:(t + 1) * P],
                                      w2_s[e % 2][:, f, :], start=f == 0, stop=f == FC - 1)
                    last.then_inc(s["y_made"], 1)

                if e == 0:
                    chunk(0)
                with pe.Fori(int(e == 0), NT // 4) as i:
                    chunk(i)

            pe.wait_ge(s["gates_ready"], 1)
            pe.wait_ge(s["ffn_b_loaded"], 16 * (1 + NT // 2))
            for a in range(2):
                last = nc.tensor.transpose(bank[:, 5, a * P:(a + 1) * P],
                                           gates[:, a * NT // 2:(a + 1) * NT // 2, :].rearrange("p t e -> p (t e)"),
                                           ident)
            last.then_inc(s["gT_made"], 1)
            pe.wait_ge(s["gT_copied"], 1)
            for b in range(B):
                o = (xc, sq)[b % 2][:].rearrange("p t c -> p (t c)")
                pe.wait_ge(s["att_ready"], b + 1)
                if b >= 2:
                    pe.wait_ge(s["out_ready"], b - 1)
                for t0 in range(0, T, 4):
                    ps = pair[b % 2][:, t0 * C:(t0 + 4) * C]
                    bt = (b % 2) * T + t0
                    mm(ps, gT[:, b // 2, :], b2_blk[:, bt:bt + 4, :].rearrange("p t c -> p (t c)"),
                       start=True, stop=False)
                    for t in range(4):
                        last = mm(ps[:, t * C:(t + 1) * C], o[:, (t0 + t) * P:(t0 + t + 1) * P], w_proj[:, 5, :],
                                  start=False, stop=t == 3)
                last.then_inc(s["proj_made"], 1)


def kernel(L0_attn_x, L0_attn_Wq, L0_attn_Wk, L0_attn_Wv, L0_attn_Wo, L0_ffn_router_w, L0_ffn_w1, L0_ffn_b1,
           L0_ffn_w2, L0_ffn_b2):
    import numpy as np
    import concourse.bacc as bacc
    from concourse.bass_utils import run_bass_kernel_spmd

    swap = [h * DH + (d + DH // 2) % DH for h in range(H) for d in range(DH)]
    lay = np.ascontiguousarray
    wq, wk, wv, wo = (np.asarray(w) for w in (L0_attn_Wq, L0_attn_Wk, L0_attn_Wv, L0_attn_Wo))
    inv_freq = (1.0 / np.float32(10000.0) ** (np.arange(0, DH, 2, dtype=np.float32) / DH)).astype(np.float32)
    angle = np.outer(np.arange(S, dtype=np.float32), inv_freq).astype(np.float32)
    angle = np.concatenate([angle, angle], axis=1).T
    sign = np.where(np.arange(DH) < DH // 2, -1.0, 1.0)[:, None]
    consts = np.zeros((P, 2 * P + E), np.float32)
    consts[:, 0:P] = np.eye(P)
    consts[:, P:2 * P] = np.triu(np.full((P, P), -BIG), k=1)
    consts[:, 2 * P:] = np.arange(E) - E
    arrays = {
        "x": lay(np.asarray(L0_attn_x).reshape(B * S, C)),
        "wq": lay(wq.T), "wqs": lay(wq[swap].T), "wk": lay(wk.T), "wks": lay(wk[swap].T),
        "wv": lay(wv.T), "wo": lay(wo.T),
        "router": lay(np.asarray(L0_ffn_router_w).T),
        "w1": lay(np.asarray(L0_ffn_w1).transpose(0, 2, 1)),
        "b1": lay(np.asarray(L0_ffn_b1).reshape(E, FC, P).transpose(2, 0, 1)),
        "w2": lay(np.asarray(L0_ffn_w2).transpose(0, 2, 1).reshape(E, FC, P, C).transpose(0, 2, 1, 3)),
        "b2": lay(np.asarray(L0_ffn_b2)),
        "cos_t": lay(np.cos(angle).astype(np.float32)),
        "sin_t": lay((np.sin(angle) * sign).astype(np.float32)),
        "consts": consts,
    }
    nc = bacc.Bacc("TRN2", target_bir_lowering=False, num_devices=1)
    args = [nc.dram_tensor(f"in_{n}", a.shape, mybir.dt.from_np(a.dtype), kind="ExternalInput").ap()
            for n, a in arrays.items()]
    args.append(nc.dram_tensor("out_0", (B * S, C), F32, kind="ExternalOutput").ap())
    args.append(nc.dram_tensor("parts_d", (2, PARTS, UNITS, HG * DH, S), BF16, kind="Internal").ap())
    args.append(nc.dram_tensor("heads_d", (UNITS, HG, DH + 1, S), F32, kind="Internal").ap())
    block_program(nc, *args)
    r = run_bass_kernel_spmd(nc, [{f"in_{n}": a for n, a in arrays.items()}], core_ids=[0])
    return r.results[0]["out_0"].reshape(B, S, C)
```

```python
from contextlib import ExitStack

import concourse.bass as bass
from concourse import mybir

F32 = mybir.dt.float32
BF16 = mybir.dt.bfloat16
ACT = mybir.ActivationFunctionType
ALU = mybir.AluOpType
AX_X = mybir.AxisListType.X

P = 128
B, S, C = 4, 1024, 128
T = S // P
NT = B * T
H, DH = 16, 8
HG = 4
G = H // HG
UNITS = B * G
E, F = 8, 512
FC = F // P
HALF = 512
PARTS = 3
KROWS = PARTS * PARTS * DH
KALL = KROWS + 2
SCALE = DH ** -0.5
BIG = 1e30
EPS = 1e-5


class Steps:

    def __init__(self, eng, sem, base=0):
        self.eng, self.sem, self.base, self.n = eng, sem, base, 0

    def done(self, ins):
        ins.then_inc(self.sem, 1)
        self.n += 1

    def settle(self):
        self.eng.wait_ge(self.sem, self.base + self.n)


def past(n):
    return not (isinstance(n, int) and n == 0)


def more(u, n):
    return not isinstance(u, int) or u + n < UNITS


def all_units(eng, unit):
    for r in range(G):
        unit(r, r)
    with eng.Fori(1, B - 1) as b:
        for r in range(G):
            unit(b * G + r, r)
    for r in range(G):
        unit(UNITS - G + r, r)


def max_items():
    items = [(0, [0, 1, 2, 3], P), (1, [0, 1, 2, 3], 2 * P)]
    items += [(qb, hs, HALF) for qb in (2, 3) for hs in ([0, 1], [2, 3])]
    items += [(qb, [h], 2 * HALF) for qb in range(4, T) for h in range(HG)]
    return items


def attention_steps():
    return [(c, kb, max(0, kb - 4 * c) * P) for c in range(2) for kb in range(4 * c + 4)]


def plan_items(items, steps, first, turn):
    cols = [HG * (HALF - q0) for _, _, q0 in steps]
    ns = len(steps)
    places = [(2, j) for j in range(first, ns)] + [(1, j) for j in range(turn)]
    act = [HG * 190 + cols[(j + 2) % ns] / 1.2 for j in range(ns)]
    room = [1.25 * act[j] - cols[(j + 2) % ns] / 2.4 - cols[j] / 2.2 for _, j in places]
    room = [max(r, 0.0) for r in room]
    weight = [len(hs) * ((qb + 1) * P + P) for qb, hs, _ in items]
    plan = [[] for _ in steps]
    n, spent, total, given = 0, 0.0, float(sum(weight)), 0.0
    for (ahead, j), r in zip(places, room):
        given += r / sum(room) * total
        while n < len(items) and spent + weight[n] / 2 <= given + 1e-6:
            plan[j].append((ahead, n))
            spent += weight[n]
            n += 1
    assert n == len(items)
    return plan


def block_program(nc, x, wq, wqs, wk, wks, wv, wo, router, w1, b1, w2, b2, cos_t, sin_t, consts, out,
                  parts_d, heads_d):
    ctx = ExitStack()
    with ctx:
        def sb(name, shape, dt=F32):
            return ctx.enter_context(nc.sbuf_tensor(name, shape, dt))

        def psum(name, shape):
            return ctx.enter_context(nc.psum_tensor(name, shape, F32))

        def sem(name):
            return ctx.enter_context(nc.semaphore(name))

        ITEMS, STEPS = max_items(), attention_steps()
        NI, NS = len(ITEMS), len(STEPS)
        MI = NI + 1

        x_all = sb("x_all", [P, NT, C])
        xn = sb("xn", [P, T, C])
        xc = sb("xc", [P, T, C])
        sq = sb("sq", [P, T, C])
        xnT = sb("xnT", [P, S])
        xnT_all = sb("xnT_all", [P, B * S])
        tq = sb("tq", [P, S])
        tk = sb("tk", [P, S])
        qr = sb("qr", [P, S])
        kr = sb("kr", [P, S])
        qsplit = sb("qsplit", [P, PARTS, S], BF16)
        ksplit = sb("ksplit", [P, PARTS, S], BF16)
        tabs = sb("tabs", [P, 2, S])
        cos_s, sin_s = tabs[:, 0, :], tabs[:, 1, :]
        w_proj = sb("w_proj", [P, 6, C])
        w_router = sb("w_router", [P, E])
        stat = sb("stat", [P, 4, T])
        v_all = sb("v_all", [P, UNITS, T, HG * DH])
        logits = sb("logits", [P, NT, E])
        r_a = xnT[:, 0 * NT * E:1 * NT * E].rearrange("p (t e) -> p t e", e=E)
        r_b = sb("r_b", [P, NT, E])
        one1 = xnT[:, 1 * NT * E:2 * NT * E].rearrange("p (t e) -> p t e", e=E)
        one2 = xnT[:, 2 * NT * E:3 * NT * E].rearrange("p (t e) -> p t e", e=E)
        gates = sb("gates", [P, NT, E])
        r_s = sb("r_s", [P, 4, NT])
        const_s = sb("const_s", [P, 2 * P + E])
        ident = const_s[:, 0:P]
        em8 = const_s[:, 2 * P:2 * P + E]
        ident_b = sb("ident_b", [P, P], BF16)
        mask_b = sb("mask_b", [P, P], BF16)
        eps_s = sb("eps_s", [P, 1])
        qstk = [sb(f"qstk{i}", [KALL, HG, S], BF16) for i in range(4)]
        kstk = [sb(f"kstk{i}", [KALL, HG, S], BF16) for i in range(4)]
        probs = [sb(f"probs{i}", [P, HG, HALF]) for i in range(3)]
        vst = [sb(f"vst{i}", [P, T, HG, 32]) for i in range(2)]
        oraw = [qsplit[:].rearrange("p a s -> p (a s)").bitcast(F32)[:, i * HALF:(i + 1) * HALF] for i in range(2)]
        mx = [sb(f"mx{i}", [P, HG, T]) for i in range(2)]
        mneg = [sb(f"mneg{i}", [P, P], BF16) for i in range(2)]
        mrow = [sb(f"mrow{i}", [2 * HG * T, P], BF16) for i in range(2)]
        w1_s = [tq[:, 0:F], tk[:, 0:F]]
        w2_s = [t[:, 0:F].rearrange("p (f c) -> p f c", c=C) for t in (qr, kr)]
        b1_s = sb("b1_s", [P, E, FC])
        hid = tabs[:].rearrange("p a (b q) -> p (a b) q", q=HALF)
        b2_blk = v_all[:].rearrange("p u t e -> p (u t e)")[:, 0:NT // 2 * C].rearrange("p (t c) -> p t c", c=C)
        gT = ksplit[:].rearrange("p a s -> p (a s)").bitcast(F32)[:, 0:2 * P].rearrange("p (a b) -> p a b", b=P)

        bank = ctx.enter_context(nc.psum_tensor("bank", [P, 8, HALF], F32))
        pair = [bank[:, 2 * i:2 * i + 2, :].rearrange("p a b -> p (a b)") for i in range(4)]
        st = [bank[:, i, :] for i in range(3)]
        pv = bank[:, 3, :]
        ms = [pair[2], pair[3]]

        names = """x_loaded w_loaded tab_loaded const_loaded ln_step ln_centered ln_squared ln_varsum ln_std xn_ready
        xnT_made xnT_ready q_made qs_made k_made ks_made v_made logits_made v_copied logits_copied
        roped q_first q_rest k_first k_rest q_split k_split q_used qs_used k_used ks_used scratch_written
        consts_ready pool_step rt_step rt_shifted rt_exped gates_ready ones_ready
        scores_made scores_read mneg_ready
        diag_seen scoresT_made probs_made diag_masked probs_used heads_copied v_staged
        ffn_b_loaded hid_made hid_ready y_made y_added gT_made gT_copied
        rec_ready att_ready proj_made out_ready out_stored xnT_kept""".split()
        s = {n: sem(n) for n in names}
        mrow_stored = [sem(f"mrow_stored{i}") for i in range(2)]
        stack_loaded = [sem(f"stack_loaded{i}") for i in range(4)]
        heads_stored = [sem(f"heads_stored{i}") for i in range(2)]
        w1_loaded = [sem(f"w1_loaded{i}") for i in range(2)]
        heads_loaded = [sem(f"heads_loaded{i}") for i in range(2)]

        block = ctx.enter_context(nc.Block())
        LN = 3

        def st_of(n):
            return st[n % 3]

        FIRST, TURN = 8, 7
        plan = plan_items(ITEMS, STEPS, FIRST, TURN)

        @block.sync
        def _(sp):
            sp.dma_start(const_s[:], consts).then_inc(s["const_loaded"], 16)
            sp.dma_start(x_all[:, 0:T, :], x[0:S, :].rearrange("(t p) c -> p t c", p=P)).then_inc(s["x_loaded"], 16)
            for n, w in enumerate((wq, wqs, wk, wks, wv, wo)):
                sp.dma_start(w_proj[:, n, :], w).then_inc(s["w_loaded"], 16)
            sp.dma_start(w_router[:], router).then_inc(s["w_loaded"], 16)
            for tab, src in ((cos_s, cos_t), (sin_s, sin_t)):
                for h in range(H):
                    sp.dma_start(tab[h * DH:(h + 1) * DH, :], src).then_inc(s["tab_loaded"], 16)
            sp.wait_ge(s["x_loaded"], 16)
            for b in range(1, B):
                sp.dma_start(x_all[:, b * T:(b + 1) * T, :],
                             x[b * S:(b + 1) * S, :].rearrange("(t p) c -> p t c", p=P)).then_inc(s["x_loaded"], 16)
                sp.wait_ge(s["x_loaded"], 16 * (b + 1))
            sp.dma_start(b1_s[:], b1).then_inc(s["ffn_b_loaded"], 16)

            def sequence(b):
                for n, (ready, tile) in enumerate(((s["q_split"], qsplit), (s["k_split"], ksplit))):
                    sp.wait_ge(ready, b + 1)
                    sp.dma_start(parts_d[n, :, bass.ds(b * G, G), :, :].rearrange("a g r s -> (g r) a s"),
                                 tile[:]).then_inc(s["scratch_written"], 16)

            sequence(0)
            with sp.Fori(1, B) as b:
                sequence(b)
            sp.wait_ge(s["scratch_written"], 32 * B)

            def load_stacks(u, par):
                for a in range(PARTS):
                    for r in range(PARTS):
                        at = (a * PARTS + r) * DH
                        for n, stk, part in ((0, qstk[par], a), (1, kstk[par], r)):
                            src = parts_d[n, part, bass.ds(u, 1), :, :]
                            sp.dma_start(stk[at:at + DH, :, :], src.rearrange("o (h d) s -> (o d) h s", d=DH)
                                         ).then_inc(stack_loaded[par], 16)

            def store_max_rows(u, par):
                sp.wait_ge(s["scores_read"], (u + 1) * MI)
                for n in range(2):
                    sp.dma_start(qstk[par][KROWS + n:KROWS + n + 1, :, :].rearrange("o h (t q) -> o (h t) q", q=P),
                                 mrow[par % 2][n * HG * T:(n + 1) * HG * T, :]).then_inc(mrow_stored[par % 2], 16)

            def store_heads(u, c):
                sp.wait_ge(s["heads_copied"], 2 * u + c + 1)
                for h in range(HG):
                    sp.dma_start(heads_d[bass.ds(u, 1), h, :, c * HALF:(c + 1) * HALF].rearrange("u r q -> (u r) q"),
                                 oraw[c][32 * h:32 * h + DH + 1, :]).then_inc(heads_stored[c], 16)

            def unit(u, r):
                if more(u, 3):
                    if past(u):
                        sp.wait_ge(s["scoresT_made"], u * (NS * HG))
                    load_stacks(u + 3, (r + 3) % 4)
                store_heads(u, 0)
                if more(u, 1):
                    store_max_rows(u + 1, (r + 1) % 4)
                store_heads(u, 1)

            def load_expert(e):
                sp.dma_start(w1_s[e % 2][:], w1[e]).then_inc(w1_loaded[e % 2], 16)
                sp.dma_start(w2_s[e % 2][:], w2[e]).then_inc(w1_loaded[e % 2], 16)

            load_expert(0)
            load_expert(1)
            for u in range(3):
                load_stacks(u, u)
            store_max_rows(0, 0)
            all_units(sp, unit)
            sp.wait_ge(s["ones_ready"], 1)
            for t in range(NT // 2):
                sp.dma_start(b2_blk[t * E:(t + 1) * E, t, :], b2).then_inc(s["ffn_b_loaded"], 16)

            for e in range(2, E):
                sp.wait_ge(s["y_made"], B * 2 * (e - 1))
                load_expert(e)

            for b in range(B):
                o, d = (xc, sq)[b % 2], (xn, hid)[b % 2]
                for c in range(2):
                    if b == 0:
                        sp.wait_ge(heads_stored[c], 64 * UNITS)
                if b >= 2:
                    sp.wait_ge(s["proj_made"], b - 1)
                if b == 1:
                    sp.wait_ge(s["y_made"], 2 * B * E)
                for h in range(H):
                    u = b * G + h // HG
                    sp.dma_start(o[h * DH:(h + 1) * DH, :, :].rearrange("p t c -> p (t c)"),
                                 heads_d[u, h % HG, 0:DH, :]).then_inc(heads_loaded[b % 2], 16)
                    dv = d[:, :, :].rearrange("p t c -> p (t c)")
                    sp.dma_start(dv[h * DH:(h + 1) * DH, 0:S],
                                 heads_d[u, h % HG, DH:DH + 1, :].broadcast_to([DH, S])
                                 ).then_inc(heads_loaded[b % 2], 16)
            for b in range(B):
                sp.wait_ge(s["out_ready"], b + 1)
                sp.dma_start(out[b * S:(b + 1) * S, :].rearrange("(t p) c -> p t c", p=P),
                             x_all[:, b * T:(b + 1) * T, :]).then_inc(s["out_stored"], 16)
            sp.wait_ge(s["out_stored"], 16 * B)

        @block.gpsimd
        def _(pool):
            k = Steps(pool, s["pool_step"])
            for i in range(4):
                k.done(pool.memset(kstk[i][64:KALL, :, :], 1.0))
                k.settle()
            for i in range(2):
                k.done(pool.memset(mneg[i][:], 0.0))
                k.settle()
                k.done(pool.memset(vst[i][:], 0.0))
                k.settle()
                k.done(pool.memset(vst[i][:, :, :, DH:DH + 1], 1.0))
                k.settle()
            k.done(pool.memset(eps_s[:], EPS))
            k.settle()
            pool.wait_ge(s["const_loaded"], 16)
            k.done(pool.tensor_copy(ident_b[:], const_s[:, 0:P]))
            k.settle()
            k.done(pool.tensor_copy(mask_b[:], const_s[:, P:2 * P]))
            k.settle()
            pool.sem_inc(s["consts_ready"], 1)
            def sequence(b):
                pool.wait_ge(s["xnT_ready"], b + 1)
                pool.tensor_copy(xnT_all[:, bass.ds(b * S, S)], xnT[:]).then_inc(s["xnT_kept"], 1)

            sequence(0)
            with pool.Fori(1, B) as b:
                sequence(b)

            def stage_v(u, par):
                pool.tensor_copy(vst[par][:, :, :, 0:DH],
                                 v_all[:, bass.ds(u, 1), :, :].rearrange("p o t (h d) -> p (o t) h d", d=DH)
                                 ).then_inc(s["v_staged"], 1)

            def unit(u, r):
                if more(u, 1):
                    if past(u):
                        pool.wait_ge(s["probs_used"], u * NS)
                    stage_v(u + 1, (r + 1) % 2)
                for n, (c, kb, q0) in enumerate(STEPS):
                    if kb >= 4 * c:
                        pool.wait_ge(s["probs_made"], (u * NS + n + 1) * HG)
                        pool.sem_inc(s["diag_seen"], 1)
                        t = probs[n % 3][:, :, q0:q0 + P]
                        pool.affine_select(out=t, in_=t, compare_op=ALU.is_ge, fill=0.0, base=0,
                                           pattern=[[0, HG], [1, P]], channel_multiplier=-1
                                           ).then_inc(s["diag_masked"], 1)

            pool.wait_ge(s["v_copied"], B)
            stage_v(0, 0)
            all_units(pool, unit)
            pool.wait_ge(s["v_staged"], UNITS)
            pool.memset(b2_blk, 0.0).then_inc(s["ones_ready"], 1)

        @block.scalar
        def _(act):
            act.wait_ge(s["consts_ready"], 1)
            def sequence(b):
                act.wait_ge(s["ln_centered"], b + 1)
                nc.scalar.activation(sq[:], xc[:], ACT.Square).then_inc(s["ln_squared"], 1)
                act.wait_ge(s["ln_varsum"], b + 1)
                nc.scalar.activation(stat[:, 2, :], stat[:, 1, :], ACT.Sqrt, bias=eps_s[:], scale=1.0 / C
                                     ).then_inc(s["ln_std"], 1)
                act.wait_ge(s["xnT_made"], b + 1)
                if past(b):
                    act.wait_ge(s["logits_made"], b)
                    act.wait_ge(s["xnT_kept"], b)
                nc.scalar.copy(xnT[:], pair[0]).then_inc(s["xnT_ready"], 1)
                if past(b):
                    act.wait_ge(s["scratch_written"], 32 * b)
                act.wait_ge(s["roped"], 2 * b + 1)
                nc.scalar.copy(qsplit[:, 0, :], qr[:]).then_inc(s["q_first"], 1)
                act.wait_ge(s["roped"], 2 * b + 2)
                nc.scalar.copy(ksplit[:, 0, :], kr[:]).then_inc(s["k_first"], 1)
                act.wait_ge(s["v_made"], b + 1)
                nc.scalar.copy(v_all[:, bass.ds(b * G, G), :, :].rearrange("p g t e -> p t g e"),
                               pair[1].rearrange("p (t g e) -> p t g e", t=T, g=G)).then_inc(s["v_copied"], 1)
                act.wait_ge(s["q_rest"], b + 1)
                nc.scalar.copy(qsplit[:, 1, :], qr[:]).then_inc(s["q_first"], 1)
                act.wait_ge(s["k_rest"], b + 1)
                nc.scalar.copy(ksplit[:, 1, :], kr[:]).then_inc(s["k_first"], 1)
                act.wait_ge(s["logits_made"], b + 1)
                nc.scalar.copy(logits[:, bass.ds(b * T, T), :],
                               pair[2][:, 0:T * E].rearrange("p (t e) -> p t e", e=E)).then_inc(s["logits_copied"], 1)

            sequence(0)
            with act.Fori(1, B) as b:
                sequence(b)
            act.wait_ge(s["rt_shifted"], 1)
            nc.scalar.activation(r_b[:], r_a, ACT.Exp).then_inc(s["rt_exped"], 1)

            def unit(u, lead):
                for n, (c, kb, q0) in enumerate(STEPS):
                    if n >= 3 or not lead:
                        act.wait_ge(s["probs_used"], u * NS + n - 2)
                    for h in range(HG):
                        at = n * HG + h
                        act.wait_ge(s["scoresT_made"], u * (NS * HG) + at + 1)
                        nc.scalar.activation(probs[n % 3][:, h, q0:HALF], st_of(at)[:, 0:HALF - q0], ACT.Exp,
                                             scale=SCALE).then_inc(s["probs_made"], 1)

            unit(0, True)
            with act.Fori(1, UNITS) as u:
                unit(u, False)

            for e in range(E):
                if e == 0:
                    act.wait_ge(s["ffn_b_loaded"], 16 * (1 + NT // 2))
                def chunk(i, e=e):
                    n = e * (NT // 4) + i
                    if past(n):
                        act.wait_ge(s["y_made"], n)
                    for f in range(FC):
                        act.wait_ge(s["hid_made"], n * FC + f + 1)
                        nc.scalar.activation(hid[:, f, :], bank[:, f, :], ACT.Relu, bias=b1_s[:, e, f:f + 1]
                                             ).then_inc(s["hid_ready"], 1)

                if e == 0:
                    chunk(0)
                with act.Fori(int(e == 0), NT // 4) as i:
                    chunk(i)

        @block.vector
        def _(dve):
            v = nc.vector
            dve.wait_ge(s["tab_loaded"], 16 * 2 * H)
            def sequence(b):
                k = Steps(dve, s["ln_step"], b * LN)
                xb = x_all[:, bass.ds(b * T, T), :]
                dve.wait_ge(s["x_loaded"], 16 * (b + 1))
                if past(b):
                    k.settle()
                k.done(v.reduce_sum(stat[:, 0, :], xb, AX_X))
                k.settle()
                k.done(v.tensor_scalar(stat[:, 3, :], stat[:, 0, :], 1.0 / C, None, ALU.mult))
                k.settle()
                v.tensor_tensor(xc[:], xb, stat[:, 3, :].unsqueeze(2).broadcast_to([P, T, C]), ALU.subtract
                                ).then_inc(s["ln_centered"], 1)
                dve.wait_ge(s["ln_squared"], b + 1)
                v.reduce_sum(stat[:, 1, :], sq[:], AX_X).then_inc(s["ln_varsum"], 1)
                dve.wait_ge(s["ln_std"], b + 1)
                k.done(v.reciprocal(stat[:, 3, :], stat[:, 2, :]))
                k.settle()
                dve.wait_ge(s["ln_centered"], b + 1)
                if past(b):
                    dve.wait_ge(s["xnT_made"], b)
                v.tensor_tensor(xn[:], xc[:], stat[:, 3, :].unsqueeze(2).broadcast_to([P, T, C]), ALU.mult
                                ).then_inc(s["xn_ready"], 1)
                for made, mades, used, useds, ps, pss, t, r in (
                        ("q_made", "qs_made", "q_used", "qs_used", pair[1], pair[2], tq, qr),
                        ("k_made", "ks_made", "k_used", "ks_used", pair[3], pair[0], tk, kr)):
                    dve.wait_ge(s[made], b + 1)
                    if past(b):
                        dve.wait_ge(s["q_split" if t is tq else "k_split"], b)
                    v.tensor_tensor(t[:], ps, cos_s[:], ALU.mult).then_inc(s[used], 1)
                    dve.wait_ge(s[mades], b + 1)
                    v.tensor_tensor(r[:], pss, sin_s[:], ALU.mult).then_inc(s[useds], 1)
                    dve.wait_ge(s[used], b + 1)
                    dve.wait_ge(s[useds], b + 1)
                    v.tensor_tensor(r[:], r[:], t[:], ALU.add).then_inc(s["roped"], 1)
                for first, rest, split, r, parts, n in (("q_first", "q_rest", "q_split", qr, qsplit, 1),
                                                        ("k_first", "k_rest", "k_split", kr, ksplit, 2)):
                    dve.wait_ge(s["roped"], 2 * b + n)
                    dve.wait_ge(s[first], 2 * b + 1)
                    v.tensor_tensor(r[:], r[:], parts[:, 0, :], ALU.subtract).then_inc(s[rest], 1)
                for first, rest, split, r, parts in (("q_first", "q_rest", "q_split", qr, qsplit),
                                                     ("k_first", "k_rest", "k_split", kr, ksplit)):
                    dve.wait_ge(s[first], 2 * b + 2)
                    dve.wait_ge(s[rest], b + 1)
                    v.tensor_tensor(parts[:, 2, :], r[:], parts[:, 1, :], ALU.subtract).then_inc(s[split], 1)
                assert k.n == LN

            sequence(0)
            with dve.Fori(1, B) as b:
                sequence(b)

            k = Steps(dve, s["rt_step"])

            def wide(col):
                return r_s[:, col, :].unsqueeze(2).broadcast_to([P, NT, E])

            em = em8.unsqueeze(1).broadcast_to([P, NT, E])
            dve.wait_ge(s["logits_copied"], B)
            dve.wait_ge(s["xnT_kept"], B)
            k.done(v.reduce_max(r_s[:, 0, :], logits[:], AX_X))
            k.settle()
            v.tensor_tensor(r_a, logits[:], wide(0), ALU.subtract).then_inc(s["rt_shifted"], 1)
            dve.wait_ge(s["rt_exped"], 1)
            k.done(v.reduce_sum(r_s[:, 1, :], r_b[:], AX_X))
            k.settle()
            k.done(v.reciprocal(r_s[:, 0, :], r_s[:, 1, :]))
            k.settle()
            k.done(v.tensor_tensor(r_b[:], r_b[:], wide(0), ALU.mult))
            for col, one in ((2, one1), (3, one2)):
                k.settle()
                k.done(v.reduce_max(r_s[:, col, :], r_b[:], AX_X))
                k.settle()
                k.done(v.tensor_tensor(r_a, r_b[:], wide(col), ALU.is_equal))
                k.settle()
                k.done(v.tensor_tensor(r_a, r_a, em, ALU.mult))
                k.settle()
                k.done(v.tensor_reduce(r_s[:, 1, :], r_a, AX_X, ALU.min))
                k.settle()
                k.done(v.tensor_tensor(one[:], em, wide(1), ALU.is_equal))
                if col == 2:
                    k.settle()
                    k.done(v.scalar_tensor_tensor(r_b[:], one[:], -2.0, r_b[:], ALU.mult, ALU.add))
            k.settle()
            k.done(v.scalar_tensor_tensor(r_s[:, 0, :], r_s[:, 2, :], 1e-9, r_s[:, 3, :], ALU.add, ALU.add))
            k.settle()
            k.done(v.reciprocal(r_s[:, 1, :], r_s[:, 0, :]))
            for col in (2, 3):
                k.settle()
                k.done(v.tensor_tensor(r_s[:, col, :], r_s[:, col, :], r_s[:, 1, :], ALU.mult))
            k.settle()
            k.done(v.tensor_tensor(gates[:], one1, wide(2), ALU.mult))
            k.done(v.tensor_tensor(r_b[:], one2, wide(3), ALU.mult))
            k.settle()
            v.tensor_tensor(gates[:], gates[:], r_b[:], ALU.add).then_inc(s["gates_ready"], 1)

            dve.wait_ge(s["consts_ready"], 1)
            def read_item(u, r, n):
                qb, hs, step = ITEMS[n]
                w = (qb + 1) * P
                at = ms[(r * MI + n) % 2]
                dve.wait_ge(s["scores_made"], u * MI + n + 1)
                src = at[:, 0:w] if len(hs) == 1 else at[:, 0:len(hs) * step].rearrange(
                    "p (h w) -> p h w", w=step)[:, :, 0:w]
                v.reduce_max(mx[r % 2][:, hs[0]:hs[-1] + 1, qb], src, AX_X).then_inc(s["scores_read"], 1)

            def split_max(u, r):
                dve.wait_ge(s["scores_read"], u * MI + NI)
                m = mx[r % 2][:].rearrange("p h t -> p (h t)")
                w = HG * T
                neg = mneg[r % 2]
                v.tensor_scalar(neg[:, 0:w], m, -1.0, None, ALU.mult).then_inc(s["mneg_ready"], 1)
                dve.wait_ge(s["mneg_ready"], 2 * u + 1)
                v.scalar_tensor_tensor(neg[:, w:2 * w], m, -1.0, neg[:, 0:w], ALU.mult, ALU.subtract
                                       ).then_inc(s["mneg_ready"], 1)

            def copy_rows(u, r):
                dve.wait_ge(s["scores_made"], u * MI + MI)
                dve.wait_ge(s["mneg_ready"], 2 * u + 2)
                if not isinstance(u, int) or u >= 2:
                    dve.wait_ge(mrow_stored[r % 2], 16 * u if r % 2 == 0 else 16 * (u - 1))
                src = ms[(r * MI + NI) % 2][0:2 * HG * T, 0:P // 2].bitcast(BF16)
                v.tensor_copy(mrow[r % 2][:], src).then_inc(s["scores_read"], 1)

            def heads_out(u, c):
                dve.wait_ge(s["probs_used"], u * NS + (4, NS)[c])
                if past(u):
                    dve.wait_ge(heads_stored[c], 64 * u)
                v.tensor_copy(oraw[c], pv).then_inc(s["heads_copied"], 1)

            def unit(u, r):
                for j in range(NS):
                    for ahead, n in plan[j]:
                        if more(u, ahead):
                            read_item(u + ahead, (r + ahead) % 4, n)
                    if j == TURN - 1 and more(u, 1):
                        split_max(u + 1, (r + 1) % 4)
                    if j == TURN and more(u, 1):
                        copy_rows(u + 1, (r + 1) % 4)
                    if j == 3:
                        heads_out(u, 0)
                    if j == NS - 1:
                        heads_out(u, 1)

            for n in range(NI):
                read_item(0, 0, n)
            split_max(0, 0)
            copy_rows(0, 0)
            for j in range(FIRST, NS):
                for _, n in plan[j]:
                    read_item(1, 1, n)
            all_units(dve, unit)

            for e in range(E):
                def chunk(i, e=e):
                    n = e * (NT // 4) + i
                    dve.wait_ge(s["y_made"], n + 1)
                    if past(n):
                        dve.wait_ge(s["y_added"], n * 4)
                    for t in range(4):
                        xt = x_all[:, bass.ds(i * 4 + t, 1), :].rearrange("p o c -> p (o c)")
                        v.scalar_tensor_tensor(xt, bank[:, 4, t * C:(t + 1) * C],
                                               gates[:, bass.ds(i * 4 + t, 1), e], xt, ALU.mult, ALU.add
                                               ).then_inc(s["y_added"], 1)

                if e == 0:
                    chunk(0)
                with dve.Fori(int(e == 0), NT // 4) as i:
                    chunk(i)
            dve.wait_ge(s["gT_made"], 1)
            v.tensor_copy(gT.rearrange("p a b -> p (a b)"), bank[:, 5, 0:2 * P]).then_inc(s["gT_copied"], 1)
            for b in range(B):
                o, d = (xc, sq)[b % 2], (xn, hid)[b % 2]
                o2 = o[:].rearrange("p t c -> p (t c)")
                d2 = d[:].rearrange("p t c -> p (t c)")[:, 0:S]
                dve.wait_ge(heads_loaded[b % 2], 16 * 2 * H * (b // 2 + 1))
                v.reciprocal(d2, d2).then_inc(s["rec_ready"], 1)
                dve.wait_ge(s["rec_ready"], b + 1)
                v.tensor_tensor(o2, o2, d2, ALU.mult).then_inc(s["att_ready"], 1)
                dve.wait_ge(s["proj_made"], b + 1)
                if b == 0:
                    dve.wait_ge(s["y_added"], NT * E)
                xt = x_all[:, b * T:(b + 1) * T, :].rearrange("p t c -> p (t c)")
                v.tensor_tensor(xt, pair[b % 2], xt, ALU.add).then_inc(s["out_ready"], 1)

        @block.tensor
        def _(pe):
            mm = nc.tensor.matmul
            pe.wait_ge(s["const_loaded"], 16)
            pe.wait_ge(s["w_loaded"], 16 * 7)
            def sequence(b):
                pe.wait_ge(s["xn_ready"], b + 1)
                if past(b):
                    pe.wait_ge(s["ks_used"], b)
                for t in range(T):
                    last = nc.tensor.transpose(pair[0][:, t * P:(t + 1) * P], xn[:, t, :], ident)
                last.then_inc(s["xnT_made"], 1)
                pe.wait_ge(s["xnT_ready"], b + 1)
                for w, ps, made, free in ((0, 1, "q_made", "v_copied"), (1, 2, "qs_made", "logits_copied"),
                                          (2, 3, "k_made", "k_used"), (3, 0, "ks_made", None)):
                    if free and past(b):
                        pe.wait_ge(s[free], b)
                    for c in range(2):
                        last = mm(pair[ps][:, c * HALF:(c + 1) * HALF], w_proj[:, w, :],
                                  xnT[:, c * HALF:(c + 1) * HALF], start=True, stop=True)
                    last.then_inc(s[made], 1)
                pe.wait_ge(s["q_used"], b + 1)
                for t in range(T):
                    last = mm(pair[1][:, t * C:(t + 1) * C], xnT[:, t * P:(t + 1) * P], w_proj[:, 4, :],
                              start=True, stop=True)
                last.then_inc(s["v_made"], 1)
                pe.wait_ge(s["qs_used"], b + 1)
                for t in range(T):
                    last = mm(pair[2][:, t * E:(t + 1) * E], xnT[:, t * P:(t + 1) * P], w_router[:],
                              start=True, stop=True)
                last.then_inc(s["logits_made"], 1)

            sequence(0)
            with pe.Fori(1, B) as b:
                sequence(b)

            def score_item(u, r, n):
                qb, hs, step = ITEMS[n]
                w = (qb + 1) * P
                at = ms[(r * MI + n) % 2]
                if not (isinstance(u, int) and u * MI + n < 2):
                    pe.wait_ge(s["scores_read"], u * MI + n - 1)
                for i, h in enumerate(hs):
                    lhsT = qstk[r][0:KROWS, h, qb * P:(qb + 1) * P]
                    for k0 in range(0, w, HALF):
                        k1 = min(w, k0 + HALF)
                        mm(at[:, i * step + k0:i * step + k1], lhsT, kstk[r][0:KROWS, h, k0:k1],
                           start=True, stop=k1 < w)
                    last = mm(at[:, i * step + qb * P:i * step + w], ident_b[:], mask_b[:], start=False, stop=True)
                last.then_inc(s["scores_made"], 1)

            def turn_max(u, r):
                pe.wait_ge(s["mneg_ready"], 2 * u + 2)
                pe.wait_ge(s["scores_read"], u * MI + NI - 1)
                nc.tensor.transpose(ms[(r * MI + NI) % 2][:, 0:P // 2].bitcast(BF16), mneg[r % 2][:],
                                    ident_b[:]).then_inc(s["scores_made"], 1)

            def score(u, r, n, h):
                c, kb, q0 = STEPS[n]
                at = n * HG + h
                if not (isinstance(u, int) and u * NS * HG + at < 3):
                    pe.wait_ge(s["probs_made"], u * (NS * HG) + at - 2)
                mm(st_of(at)[:, 0:HALF - q0], kstk[r][:, h, kb * P:(kb + 1) * P],
                   qstk[r][:, h, c * HALF + q0:(c + 1) * HALF], start=True, stop=True
                   ).then_inc(s["scoresT_made"], 1)

            def products(u, r, n):
                c, kb, q0 = STEPS[n]
                if n == 0:
                    pe.wait_ge(s["v_staged"], u + 1)
                if kb == 0 and (c or past(u)):
                    pe.wait_ge(s["heads_copied"], 2 * u + c)
                pe.wait_ge(s["probs_made"], u * (NS * HG) + (n + 1) * HG)
                if kb >= 4 * c:
                    pe.wait_ge(s["diag_masked"], u * 8 + c * 4 + (kb - 4 * c) + 1)
                for h in range(HG):
                    last = mm(pv[32 * h:32 * h + 32, q0:HALF], vst[r % 2][:, kb, h, :], probs[n % 3][:, h, q0:HALF],
                              start=kb == 0, stop=kb == 4 * c + 3)
                last.then_inc(s["probs_used"], 1)

            LEAD = 2

            def unit(u, r):
                for j in range(NS):
                    ahead, n = divmod(j + LEAD, NS)
                    todo = [(u + a, (r + a) % 4, m) for a, m in plan[j] if more(u, a)]
                    if ahead and n == 0 and more(u, 1):
                        pe.wait_ge(mrow_stored[(r + 1) % 2], mrow_count(u + 1, r + 1))
                    if j == FIRST and more(u, 2):
                        pe.wait_ge(stack_loaded[(r + 2) % 4], stack_count(u + 2, (r + 2) % 4))
                    for h in range(HG):
                        if more(u, ahead):
                            score(u + ahead, (r + ahead) % 4, n, h)
                        if h and todo:
                            score_item(*todo.pop(0))
                    for item in todo:
                        score_item(*item)
                    if j == TURN and more(u, 1):
                        turn_max(u + 1, (r + 1) % 4)
                    products(u, r, j)

            def mrow_count(u, r):
                return 16 * (u + 2 - r % 2)

            def stack_count(u, r):
                n = 16 * 2 * PARTS * PARTS
                return (n // 4) * (u - r + 4)

            pe.wait_ge(s["v_copied"], B)
            pe.wait_ge(s["logits_copied"], B)
            pe.wait_ge(s["k_used"], B)
            pe.wait_ge(s["ks_used"], B)
            pe.wait_ge(s["consts_ready"], 1)
            pe.wait_ge(stack_loaded[0], stack_count(0, 0))
            for n in range(NI):
                score_item(0, 0, n)
            turn_max(0, 0)
            pe.wait_ge(stack_loaded[1], stack_count(1, 1))
            for j in range(FIRST, NS):
                for _, n in plan[j]:
                    score_item(1, 1, n)
            pe.wait_ge(mrow_stored[0], mrow_count(0, 0))
            for n in range(LEAD):
                for h in range(HG):
                    score(0, 0, n, h)
            all_units(pe, unit)

            pe.wait_ge(s["heads_copied"], 2 * UNITS)
            for e in range(E):
                pe.wait_ge(w1_loaded[e % 2], 32 * (e // 2 + 1))
                def chunk(i, e=e):
                    n = e * (NT // 4) + i
                    for f in range(FC):
                        mm(bank[:, f, :], w1_s[e % 2][:, f * P:(f + 1) * P], xnT_all[:, bass.ds(i * HALF, HALF)],
                           start=True, stop=True).then_inc(s["hid_made"], 1)
                    pe.wait_ge(s["hid_ready"], (n + 1) * FC)
                    if past(n):
                        pe.wait_ge(s["y_added"], n * 4)
                    for t in range(4):
                        for f in range(FC):
                            last = mm(bank[:, 4, t * C:(t + 1) * C], hid[:, f, t * P:(t + 1) * P],
                                      w2_s[e % 2][:, f, :], start=f == 0, stop=f == FC - 1)
                    last.then_inc(s["y_made"], 1)

                if e == 0:
                    chunk(0)
                with pe.Fori(int(e == 0), NT // 4) as i:
                    chunk(i)

            pe.wait_ge(s["gates_ready"], 1)
            pe.wait_ge(s["ffn_b_loaded"], 16 * (1 + NT // 2))
            for a in range(2):
                last = nc.tensor.transpose(bank[:, 5, a * P:(a + 1) * P],
                                           gates[:, a * NT // 2:(a + 1) * NT // 2, :].rearrange("p t e -> p (t e)"),
                                           ident)
            last.then_inc(s["gT_made"], 1)
            pe.wait_ge(s["gT_copied"], 1)
            for b in range(B):
                o = (xc, sq)[b % 2][:].rearrange("p t c -> p (t c)")
                pe.wait_ge(s["att_ready"], b + 1)
                if b >= 2:
                    pe.wait_ge(s["out_ready"], b - 1)
                for t0 in range(0, T, 4):
                    ps = pair[b % 2][:, t0 * C:(t0 + 4) * C]
                    bt = (b % 2) * T + t0
                    mm(ps, gT[:, b // 2, :], b2_blk[:, bt:bt + 4, :].rearrange("p t c -> p (t c)"),
                       start=True, stop=False)
                    for t in range(4):
                        last = mm(ps[:, t * C:(t + 1) * C], o[:, (t0 + t) * P:(t0 + t + 1) * P], w_proj[:, 5, :],
                                  start=False, stop=t == 3)
                last.then_inc(s["proj_made"], 1)


def kernel(L0_attn_x, L0_attn_Wq, L0_attn_Wk, L0_attn_Wv, L0_attn_Wo, L0_ffn_router_w, L0_ffn_w1, L0_ffn_b1,
           L0_ffn_w2, L0_ffn_b2):
    import numpy as np
    import concourse.bacc as bacc
    from concourse.bass_utils import run_bass_kernel_spmd

    swap = [h * DH + (d + DH // 2) % DH for h in range(H) for d in range(DH)]
    lay = np.ascontiguousarray
    wq, wk, wv, wo = (np.asarray(w) for w in (L0_attn_Wq, L0_attn_Wk, L0_attn_Wv, L0_attn_Wo))
    inv_freq = (1.0 / np.float32(10000.0) ** (np.arange(0, DH, 2, dtype=np.float32) / DH)).astype(np.float32)
    angle = np.outer(np.arange(S, dtype=np.float32), inv_freq).astype(np.float32)
    angle = np.concatenate([angle, angle], axis=1).T
    sign = np.where(np.arange(DH) < DH // 2, -1.0, 1.0)[:, None]
    consts = np.zeros((P, 2 * P + E), np.float32)
    consts[:, 0:P] = np.eye(P)
    consts[:, P:2 * P] = np.triu(np.full((P, P), -BIG), k=1)
    consts[:, 2 * P:] = np.arange(E) - E
    arrays = {
        "x": lay(np.asarray(L0_attn_x).reshape(B * S, C)),
        "wq": lay(wq.T), "wqs": lay(wq[swap].T), "wk": lay(wk.T), "wks": lay(wk[swap].T),
        "wv": lay(wv.T), "wo": lay(wo.T),
        "router": lay(np.asarray(L0_ffn_router_w).T),
        "w1": lay(np.asarray(L0_ffn_w1).transpose(0, 2, 1)),
        "b1": lay(np.asarray(L0_ffn_b1).reshape(E, FC, P).transpose(2, 0, 1)),
        "w2": lay(np.asarray(L0_ffn_w2).transpose(0, 2, 1).reshape(E, FC, P, C).transpose(0, 2, 1, 3)),
        "b2": lay(np.asarray(L0_ffn_b2)),
        "cos_t": lay(np.cos(angle).astype(np.float32)),
        "sin_t": lay((np.sin(angle) * sign).astype(np.float32)),
        "consts": consts,
    }
    nc = bacc.Bacc("TRN2", target_bir_lowering=False, num_devices=1)
    args = [nc.dram_tensor(f"in_{n}", a.shape, mybir.dt.from_np(a.dtype), kind="ExternalInput").ap()
            for n, a in arrays.items()]
    args.append(nc.dram_tensor("out_0", (B * S, C), F32, kind="ExternalOutput").ap())
    args.append(nc.dram_tensor("parts_d", (2, PARTS, UNITS, HG * DH, S), BF16, kind="Internal").ap())
    args.append(nc.dram_tensor("heads_d", (UNITS, HG, DH + 1, S), F32, kind="Internal").ap())
    block_program(nc, *args)
    r = run_bass_kernel_spmd(nc, [{f"in_{n}": a for n, a in arrays.items()}], core_ids=[0])
    return r.results[0]["out_0"].reshape(B, S, C)
```

```python
from contextlib import ExitStack

import concourse.bass as bass
from concourse import mybir

F32 = mybir.dt.float32
BF16 = mybir.dt.bfloat16
I32 = mybir.dt.int32
ACT = mybir.ActivationFunctionType
ALU = mybir.AluOpType
AX_X = mybir.AxisListType.X

P = 128
B, S, C = 4, 1024, 128
T = S // P
NT = B * T
H, DH = 16, 8
HG = 4
G = H // HG
UNITS = B * G
E, F = 8, 512
FC = F // P
HALF = 512
CK = HALF // P
PARTS = 3
KROWS = PARTS * PARTS * DH
KALL = KROWS + 2
SCALE = DH ** -0.5
BIG = 1e30
EPS = 1e-5
SLOTS = 2 * B * S
ROUND = P
TILES = SLOTS // P + E
WIDE = F + FC + F
GOT = 8
LAST = UNITS - G


class Steps:

    def __init__(self, eng, sem, base=0):
        self.eng, self.sem, self.base, self.n = eng, sem, base, 0

    def done(self, ins):
        ins.then_inc(self.sem, 1)
        self.n += 1

    def settle(self):
        self.eng.wait_ge(self.sem, self.base + self.n)


def past(n):
    return not (isinstance(n, int) and n == 0)


def more(u, n):
    return not isinstance(u, int) or u + n < UNITS


def all_units(eng, unit, between_first=None, before_last=None):
    for r in range(G):
        unit(r, r)
    if between_first:
        between_first()
    with eng.Fori(1, B - 1) as b:
        for r in range(G):
            unit(b * G + r, r)
    if before_last:
        before_last()
    for r in range(G):
        unit(LAST + r, r)


def all_tiles(eng, tile):
    for r in range(4):
        tile(r, r)
    with eng.Fori(1, TILES // 4 - 1) as i:
        for r in range(4):
            tile(i * 4 + r, r)
    for r in range(4):
        tile(TILES - 4 + r, r)


def more_sequences(b):
    return not isinstance(b, int) or b + 1 < B


def max_items():
    items = [(0, [0, 1, 2, 3], P), (1, [0, 1, 2, 3], 2 * P)]
    items += [(qb, hs, HALF) for qb in (2, 3) for hs in ([0, 1], [2, 3])]
    items += [(qb, [h], 2 * HALF) for qb in range(4, T) for h in range(HG)]
    return items


def attention_steps():
    return [(c, kb, max(0, kb - 4 * c) * P) for c in range(2) for kb in range(4 * c + 4)]


def plan_items(counts, first, turn):
    steps = len(counts)
    plan, n = [[] for _ in range(steps)], 0
    for ahead, places in ((2, range(first, steps)), (1, range(turn))):
        for j in places:
            plan[j] = [(ahead, n + i) for i in range(counts[j])]
            n += counts[j]
    return plan


def block_program(nc, x, w_projs, router, w_experts, b2, rope_t, consts, out,
                  parts_d, heads_d, slots_in_d, slots_out_d, sums_d):
    ctx = ExitStack()
    with ctx:
        def sb(name, shape, dt=F32):
            return ctx.enter_context(nc.sbuf_tensor(name, shape, dt))

        def psum(name, shape):
            return ctx.enter_context(nc.psum_tensor(name, shape, F32))

        def sem(name):
            return ctx.enter_context(nc.semaphore(name))

        ITEMS, STEPS = max_items(), attention_steps()
        NI, NS = len(ITEMS), len(STEPS)
        MI = NI + 1

        early = sb("early", [P, E * WIDE])
        x_all = early[:, 0:NT * C].rearrange("p (t c) -> p t c", c=C)
        tq, tk, qr, kr = (early[:, NT * C + i * S:NT * C + (i + 1) * S] for i in range(4))
        xn_all = sb("xn_all", [P, NT, C])
        acc = xn_all
        tiles_s = sb("tiles_s", [P, T, C])
        xn = tiles_s[:]
        staged = sb("staged", [P, 2, WIDE])
        halves = staged[:, 1, 0:6 * NT].rearrange("p (t n) -> p t n", n=6)
        mean_var = staged[:, 1, 6 * NT:8 * NT].rearrange("p (t n) -> p t n", n=2)
        std, rstd = (staged[:, 1, i * NT:(i + 1) * NT] for i in (8, 9))
        xnT = sb("xnT", [P, S])
        qsplit = sb("qsplit", [P, PARTS, S], BF16)
        ksplit = sb("ksplit", [P, PARTS, S], BF16)
        tabs = sb("tabs", [P, 2, S])
        cos_s, sin_s = tabs[:, 0, :], tabs[:, 1, :]
        b2_blk = tabs[:].rearrange("p a (t c) -> p (a t) c", c=C)
        w_proj = sb("w_proj", [P, 7, C])
        w_router = sb("w_router", [P, E])
        v_all = sb("v_all", [P, UNITS, T, HG * DH])
        logits = sb("logits", [P, NT, E])
        rt = [staged[:, 0, i * NT * E:(i + 1) * NT * E].rearrange(
            "p (t e) -> p t e", e=E) for i in range(4)]
        rt2 = [staged[:, 1, i * NT * E:(i + 1) * NT * E] for i in range(4)]
        below = xnT[:, 0:TILES * E].rearrange("p (j e) -> p j e", e=E)
        ends = xnT[:, TILES * E:TILES * (E + 1)]
        gates = logits
        share = sb("share", [P, 2, NT])
        r_s = sb("r_s", [P, 4, NT])
        r_e = sb("r_e", [P, 4, E])
        r_i = sb("r_i", [P, 2, E], I32)
        slot = sb("slot", [P, 2, NT], I32)
        expert = sb("expert", [P, TILES], I32)
        NCONST = 4 * P + E + NT * E + TILES
        const_s = sb("const_s", [P, NCONST])
        ident = const_s[:, 0:P]
        sum_rows = const_s[:, 3 * P:4 * P]
        em8 = const_s[:, 4 * P:4 * P + E]
        inner = const_s[:, 4 * P + E:4 * P + E + NT * E]
        starts = const_s[:, 4 * P + E + NT * E:NCONST]
        ident_b = sb("ident_b", [P, P], BF16)
        mask_b = sb("mask_b", [P, P], BF16)
        before_b = sb("before_b", [P, P], BF16)
        ones_b = sb("ones_b", [P, P], BF16)
        chosen_b = rt2[3].bitcast(BF16)[:, 0:NT * E]
        eps_s = sb("eps_s", [P, 1])
        table_s = sb("table_s", [P, 2])
        stacks = [sb(f"stack{i}", [P, 2, HG, S], BF16) for i in range(4)]
        qstk = [t[0:KALL, 0, :, :] for t in stacks]
        kstk = [t[0:KALL, 1, :, :] for t in stacks]
        probs = [sb(f"probs{i}", [P, HG, HALF]) for i in range(3)]
        zeros = probs[2][:, 0, 0:C]
        vst = [sb(f"vst{i}", [P, T, HG, 32]) for i in range(2)]
        oraw = [xnT[:, i * HALF:(i + 1) * HALF] for i in range(2)]
        mx = [sb(f"mx{i}", [P, HG, T]) for i in range(2)]
        mneg = [sb(f"mneg{i}", [P, P], BF16) for i in range(2)]
        mrow = [sb(f"mrow{i}", [2 * HG * T, P], BF16) for i in range(2)]
        gT = tiles_s[:, 6:8, :]
        xt = [tiles_s[:, i, :] for i in range(4)]
        xtT = [tiles_s[:, 4 + i, :] for i in range(2)]
        w_s = [staged[:, i, :] for i in range(2)]
        hid = [qsplit[:].rearrange("p a s -> p (a s)").bitcast(F32)[:, i * F:(i + 1) * F] for i in range(2)]
        yst = [ksplit[:].rearrange("p a s -> p (a s)").bitcast(F32)[:, i * C:(i + 1) * C] for i in range(4)]
        got = [ksplit[:].rearrange("p a s -> p (a s)").bitcast(F32)[:, (4 + i) * C:(5 + i) * C] for i in range(GOT)]
        late = [t[:].rearrange("p a h s -> p (a h s)").bitcast(F32) for t in stacks[0:2]]
        heads_s = [late[b // 2][:, (b % 2) * 2 * S:(b % 2) * 2 * S + S] for b in range(B)]
        over_s = [late[b // 2][:, (b % 2) * 2 * S + S:(b % 2 + 1) * 2 * S] for b in range(B)]
        sums_s = tiles_s[:, 0:B, :]
        over_last, heads_last = probs[0][:, 0, :], probs[0][:, 1, :]

        bank = ctx.enter_context(nc.psum_tensor("bank", [P, 8, HALF], F32))
        pair = [bank[:, 2 * i:2 * i + 2, :].rearrange("p a b -> p (a b)") for i in range(4)]
        st = [bank[:, i, :] for i in range(3)]
        pv = bank[:, 3, :]
        ms = [pair[2], pair[3]]

        names = """const_loaded w_loaded tab_loaded eps_ready table_loaded consts_ready pool_step
        ln_halves ln_stats ln_std ln_rstd xn_ready xn_kept xnT_made xnT_ready
        q_made qs_made k_made ks_made q_used qs_used k_used ks_used roped
        q_first q_rest k_first k_rest q_split k_split v_made v_copied logits_made logits_copied """
        names += """rt_step rt_shifted rt_exped chosen_ready counted gT_made routed
        zeros_ready slots_zeroed scattered """
        names += """scores_made scores_read mneg_ready
        scoresT_made probs_made diag_seen diag_masked probs_used v_staged heads_copied """
        names += """experts_loaded w1_free w1_staged w2_free w2_staged xT_made xT_ready
        h_made hid_low hid_high y_made y_copied
        acc_loaded b2_zeroed b2_loaded combined sums_loaded sums_inverted att_ready sums_spread over_made
        proj_made out_stored"""
        s = {n: sem(n) for n in names.split()}
        parts_written = [sem(f"{n}_parts_written") for n in "qk"]
        x_loaded = [sem(f"x_loaded{b}") for b in range(B)]
        sums_stored = [sem(f"sums_stored{b}") for b in range(B)]
        xt_loaded = [sem(f"xt_loaded{i}") for i in range(4)]
        y_stored = [sem(f"y_stored{i}") for i in range(4)]
        gathered = [sem(f"gathered{i}") for i in range(GOT)]
        late_loaded = [sem(f"late_loaded{i}") for i in range(B)]
        mrow_stored = [sem(f"mrow_stored{i}") for i in range(2)]
        stack_loaded = [sem(f"stack_loaded{i}") for i in range(4)]
        last_loaded = [sem(f"last_loaded{c}") for c in range(2)]
        heads_stored = [sem(f"heads_stored{i}") for i in range(2)]

        block = ctx.enter_context(nc.Block())

        FIRST, TURN = 8, 7
        LEAD = 2
        TILES_OF_STEP = [2, 2, 2, 2, 2, 2, 2, 0, 3, 2, 2, 1]
        plan = plan_items(TILES_OF_STEP, FIRST, TURN)
        assert sum(map(len, plan)) == NI
        AT_START = 2
        TILES_OF_STEP_0 = [2, 3, 3, 3, 3, 3, 3, 0, 0, 0, 0, 0]
        assert AT_START + sum(TILES_OF_STEP_0[:TURN]) == NI
        plan_0 = [[(1, AT_START + sum(TILES_OF_STEP_0[:j]) + i) for i in range(n)] if j < TURN else plan[j]
                  for j, n in enumerate(TILES_OF_STEP_0)]

        def plan_of(u, j):
            return (plan_0 if isinstance(u, int) and u == 0 else plan)[j]
        HALFWAY = (LAST + 1) * MI + sum(ahead == 2 for step in plan for ahead, _ in step)

        PROJECTS = {(LAST + 3, 2): 0, (LAST + 3, 5): 1, (LAST + 3, 8): 2}
        FINISHES = {(LAST + 2, 11): 0, (LAST + 3, 2): 1, (LAST + 3, 5): 2}
        INVERTS = {4: 0, 5: 1, 7: 2}
        TRANSFERS = [[1, 0, 0, 11, 2, 1, 0, 2]] * 2 + [[1, 0, 0, 12, 2, 1, 0, 2]] + [[1, 0, 0, 9, 2, 0, 0, 0]]
        COMBINES = [[0, 0, 1, 0, 1, 2, 3, 3, 2, 1, 1, 1], [0, 1, 1, 0, 2, 2, 3, 3, 2, 1, 1, 1],
                    [0, 1, 1, 0, 2, 3, 3, 3, 2, 1, 1, 1], [1, 1, 1, 0, 1, 2, 2, 2, 2, 1, 1, 0]]
        assert sum(map(sum, TRANSFERS)) == sum(map(sum, COMBINES)) == 2 * NT

        def share_of(table, r, i):
            before = sum(map(sum, table[:r])) + sum(table[r][:i])
            return range(before, before + table[r][i])

        def st_of(n):
            return st[n % 3]

        def gather_order(n):
            return n // 4 * 2 + n % 2, n // 2 % 2

        @block.sync
        def _(sp):
            def load_x(b):
                sp.dma_start(x_all[:, b * T:(b + 1) * T, :],
                             x[b * S:(b + 1) * S, :].rearrange("(t p) c -> p t c", p=P)).then_inc(x_loaded[b], 16)

            load_x(0)
            sp.dma_start(const_s[:], consts).then_inc(s["const_loaded"], 16)
            sp.dma_start(w_proj[:], w_projs).then_inc(s["w_loaded"], 16)
            sp.dma_start(w_router[:], router).then_inc(s["w_loaded"], 16)
            load_x(1)
            for n in range(2):
                sp.dma_start(tabs[:, n, :], rope_t[n:n + 1, :, :].broadcast_to([H, DH, S])
                             ).then_inc(s["tab_loaded"], 16)
            for b in range(2, B):
                load_x(b)

            def keep_rows(b):
                sp.wait_ge(s["xn_ready"], b + 1)
                sp.dma_start(xn_all[:, b * T:(b + 1) * T, :], xn).then_inc(s["xn_kept"], 16)

            def keep_parts(b):
                for n, (ready, tile) in enumerate(((s["q_split"], qsplit), (s["k_split"], ksplit))):
                    sp.wait_ge(ready, b + 1)
                    for a in range(PARTS):
                        sp.dma_start(parts_d[n, b * G:(b + 1) * G, :, a, :, :].rearrange("g h d s -> (g h) d s"),
                                     tile[:, a, :]).then_inc(parts_written[n], 16)

            def load_stacks(u, r):
                def rows(n, at, part, count):
                    src = parts_d[n, bass.ds(u, 1), :, part:part + count, :, :].rearrange("o h a d s -> (o a d) h s")
                    sp.dma_start((qstk, kstk)[n][r][at * DH:(at + count) * DH, :, :], src).then_inc(stack_loaded[r], 16)

                for turn in range(PARTS):
                    rows(1, turn * PARTS, 0, PARTS)
                    rows(0, turn * PARTS, turn, PARTS - turn)
                    if turn:
                        rows(0, turn * PARTS + PARTS - turn, 0, turn)

            def store_max_rows(u, par):
                sp.wait_ge(s["scores_read"], (u + 1) * MI)
                for n in range(2):
                    sp.dma_start(qstk[par][KROWS + n:KROWS + n + 1, :, :].rearrange("o h (t q) -> o (h t) q", q=P),
                                 mrow[par % 2][n * HG * T:(n + 1) * HG * T, :]).then_inc(mrow_stored[par % 2], 16)

            def store_heads(u, c):
                sp.wait_ge(s["heads_copied"], 2 * u + c + 1)
                for h in range(HG):
                    sp.dma_start(heads_d[bass.ds(u, 1), h, :, c * HALF:(c + 1) * HALF].rearrange("u r q -> (u r) q"),
                                 oraw[c][32 * h:32 * h + DH + 1, :]).then_inc(heads_stored[c], 16)

            def unit(u, r):
                if more(u, 3):
                    if past(u):
                        sp.wait_ge(s["scoresT_made"], u * (NS * HG))
                    load_stacks(u + 3, (r + 3) % 4)
                if isinstance(u, int) and u == 1:
                    sp.dma_start(early[:], w_experts).then_inc(s["experts_loaded"], 16)
                if isinstance(u, int) and u == 2:
                    sp.wait_ge(s["b2_zeroed"], 1)
                    for t in range(NT // 2):
                        sp.dma_start(b2_blk[t * E:(t + 1) * E, t, :], b2).then_inc(s["b2_loaded"], 16)
                if isinstance(u, int) and u == LAST + 1:
                    sp.wait_ge(heads_stored[0], 64 * LAST)
                    sp.wait_ge(heads_stored[1], 64 * LAST)
                    for b in range(B - 1):
                        load_sums(b)
                store_heads(u, 0)
                if more(u, 1):
                    store_max_rows(u + 1, (r + 1) % 4)
                if isinstance(u, int) and u == LAST + 2:
                    for b in range(B - 1):
                        store_sums(b)
                    for b in range(B - 1):
                        spread_sums(b)
                if isinstance(u, int) and u == LAST + 3:
                    load_last_sums()
                    spread_last()
                    for b in range(B - 2):
                        store_out(b)
                    return
                store_heads(u, 1)

            def load_sums(b):
                src = heads_d[b * G:(b + 1) * G, :, DH, :].rearrange("g h (k q) -> (g h) k q", q=P)
                sp.dma_start(sums_s[:, b, :], src).then_inc(s["sums_loaded"], 16)

            def store_sums(b):
                sp.wait_ge(s["sums_inverted"], b + 1)
                sp.dma_start(sums_d[b].rearrange("h (k q) -> (h k) q", q=P), sums_s[:, b, :]
                             ).then_inc(sums_stored[b], 16)

            def spread_sums(b):
                sp.wait_ge(sums_stored[b], 16)
                sp.dma_start(over_s[b], sums_d[b].unsqueeze(1).broadcast_to([H, DH, S])).then_inc(late_loaded[b], 16)
                sp.dma_start(heads_s[b], heads_d[b * G:(b + 1) * G, :, 0:DH, :].rearrange("g h d s -> (g h) d s")
                             ).then_inc(late_loaded[b], 16)

            def load_last_sums():
                sp.wait_ge(heads_stored[0], 64 * UNITS)
                sp.wait_ge(heads_stored[1], 64 * (UNITS - 1))
                for to, c, u in ((0, 0, UNITS), (CK * H, 1, UNITS - 1)):
                    src = heads_d[LAST:u, :, DH, c * HALF:(c + 1) * HALF].rearrange("g h (k q) -> (g h) k q", q=P)
                    n = (u - LAST) * HG * CK
                    sp.dma_start(sums_s[to:to + n, B - 1, :], src).then_inc(s["sums_loaded"], 16)

            def spread_last():
                sp.wait_ge(s["sums_inverted"], B)
                for to, c, u in ((0, 0, UNITS), (CK * H, 1, UNITS - 1)):
                    n = (u - LAST) * HG
                    sp.dma_start(sums_d[B - 1, 0:n, c * HALF:(c + 1) * HALF].rearrange("h (k q) -> h k q", q=P),
                                 sums_s[to:to + n * CK, B - 1, :]).then_inc(sums_stored[B - 1], 16)
                sp.wait_ge(sums_stored[B - 1], 32)
                for c, u in ((0, UNITS), (1, UNITS - 1)):
                    n, cols = (u - LAST) * HG, slice(c * HALF, (c + 1) * HALF)
                    sp.dma_start(over_s[B - 1][0:n * DH, cols], sums_d[B - 1, 0:n, cols].unsqueeze(1).broadcast_to(
                        [n, DH, HALF])).then_inc(last_loaded[c], 16)
                    sp.dma_start(heads_s[B - 1][0:n * DH, cols], heads_d[LAST:u, :, 0:DH, cols].rearrange(
                        "g h d s -> (g h) d s")).then_inc(last_loaded[c], 16)

            def store_last(c):
                sp.wait_ge(s["scores_read"], UNITS * MI + B + c)
                sp.wait_ge(s["combined"], 2 * NT)
                t0 = (B - 1) * T + c * CK
                sp.dma_start(out[t0 * P:(t0 + CK) * P, :].rearrange("(t p) c -> p t c", p=P),
                             acc[:, t0:t0 + CK, :]).then_inc(s["out_stored"], 16)

            def store_out(b):
                sp.wait_ge(s["scores_read"], UNITS * MI + b + 1)
                sp.wait_ge(s["combined"], 2 * T * (b + 1))
                sp.dma_start(out[b * S:(b + 1) * S, :].rearrange("(t p) c -> p t c", p=P),
                             acc[:, b * T:(b + 1) * T, :]).then_inc(s["out_stored"], 16)

            def load_acc():
                sp.wait_ge(s["scattered"], 16 * 2 * NT)
                sp.dma_start(acc[:], x.rearrange("(t p) c -> p t c", p=P)).then_inc(s["acc_loaded"], 16)

            def load_tile(j, r):
                sp.dma_start(xt[r], slots_in_d[bass.ds(j * P, P), :]).then_inc(xt_loaded[r], 16)

            def store_tile(j, r):
                sp.wait_ge(s["y_copied"], j + 1)
                sp.dma_start(slots_out_d[bass.ds(j * P, P), :], yst[r]).then_inc(y_stored[r], 16)

            def tile(j, r):
                if past(j):
                    store_tile(j - 1, (r - 1) % 4)
                if not isinstance(j, int) or j + 4 < TILES:
                    sp.wait_ge(s["xT_made"], j + 1)
                    load_tile(j + 4, r)

            def before_tiles():
                load_acc()
                for j in range(4):
                    load_tile(j, j)

            def experts():
                all_tiles(sp, tile)
                store_tile(TILES - 1, (TILES - 1) % 4)

            keep_rows(0)
            for b in range(B):
                if more_sequences(b):
                    keep_rows(b + 1)
                keep_parts(b)
                if b == 1:
                    sp.wait_ge(s["consts_ready"], 1)
                    for written in parts_written:
                        sp.wait_ge(written, 16 * PARTS)
                if b:
                    load_stacks(b - 1, b - 1)
            sp.wait_ge(s["zeros_ready"], 1)
            sp.dma_start(slots_in_d.rearrange("(j p) c -> p j c", p=P),
                         zeros.unsqueeze(1).broadcast_to([P, TILES, C])).then_inc(s["slots_zeroed"], 16)
            for written in parts_written:
                sp.wait_ge(written, 16 * PARTS * B)
            store_max_rows(0, 0)
            all_units(sp, unit, before_tiles, experts)
            store_out(B - 2)
            for c in range(2):
                store_last(c)
            sp.wait_ge(s["out_stored"], 16 * (B + 1))

        @block.gpsimd
        def _(pool):
            k = Steps(pool, s["pool_step"])
            pool.memset(eps_s[:], EPS).then_inc(s["eps_ready"], 1)
            pool.memset(zeros, 0.0).then_inc(s["zeros_ready"], 1)
            pool.wait_ge(s["zeros_ready"], 1)

            def split(b):
                for n, (used, used2, t, r, first, rest, parts) in enumerate((
                        ("q_used", "qs_used", tq, qr, "q_first", "q_rest", qsplit),
                        ("k_used", "ks_used", tk, kr, "k_first", "k_rest", ksplit))):
                    pool.wait_ge(s[used], b + 1)
                    pool.wait_ge(s[used2], b + 1)
                    pool.tensor_tensor(r, r, t, ALU.add).then_inc(s["roped"], 1)
                    pool.wait_ge(s["roped"], 2 * b + n + 1)
                    pool.wait_ge(s[first], 2 * b + 1)
                    pool.tensor_tensor(r, r, parts[:, 0, :], ALU.subtract).then_inc(s[rest], 1)

            pool.wait_ge(s["const_loaded"], 16)
            k.done(pool.tensor_copy(ident_b[:], ident))
            k.settle()
            k.done(pool.tensor_copy(mask_b[:], const_s[:, P:2 * P]))
            k.settle()
            k.done(pool.tensor_copy(before_b[:], const_s[:, 2 * P:3 * P]))
            k.settle()
            k.done(pool.memset(ones_b[:], 1.0))
            k.settle()
            for i in range(4):
                k.done(pool.memset(kstk[i][64:KALL, :, :], 1.0))
                k.settle()
            for i in range(2):
                k.done(pool.memset(mneg[i][:], 0.0))
                k.settle()
            pool.sem_inc(s["consts_ready"], 1)
            for i in range(2):
                k.done(pool.memset(vst[i][:], 0.0))
                k.settle()
                k.done(pool.memset(vst[i][:, :, :, DH:DH + 1], 1.0))
                k.settle()

            with pool.Fori(0, B) as b:
                split(b)
            pool.wait_ge(s["k_split"], B)
            pool.memset(b2_blk, 0.0).then_inc(s["b2_zeroed"], 1)

            def scatter(n):
                k2, t = divmod(n, NT)
                pool.indirect_dma_start(out=slots_in_d, out_offset=bass.IndirectOffsetOnAxis(
                    ap=slot[:, k2, t:t + 1], axis=0), in_=xn_all[:, t, :], in_offset=None
                    ).then_inc(s["scattered"], 16)

            def gather(n):
                t, k2 = gather_order(n)
                if n >= GOT:
                    pool.wait_ge(s["combined"], n - GOT + 1)
                pool.indirect_dma_start(out=got[n % GOT], out_offset=None, in_=slots_out_d,
                                        in_offset=bass.IndirectOffsetOnAxis(ap=slot[:, k2, t:t + 1], axis=0)
                                        ).then_inc(gathered[n % GOT], 16)

            def stage_v(u, par):
                pool.tensor_copy(vst[par][:, :, :, 0:DH],
                                 v_all[:, bass.ds(u, 1), :, :].rearrange("p o t (h d) -> p (o t) h d", d=DH)
                                 ).then_inc(s["v_staged"], 1)

            def unit(u, r):
                for n, (c, kb, q0) in enumerate(STEPS):
                    if kb >= 4 * c:
                        pool.wait_ge(s["probs_made"], (u * NS + n + 1) * HG)
                        pool.sem_inc(s["diag_seen"], 1)
                        t = probs[n % 3][:, :, q0:q0 + P]
                        pool.affine_select(out=t, in_=t, compare_op=ALU.is_ge, fill=0.0, base=0,
                                           pattern=[[0, HG], [1, P]], channel_multiplier=-1
                                           ).then_inc(s["diag_masked"], 1)
                        d = c * 4 + kb - 4 * c
                        if d == 3 and more(u, 1):
                            if past(u):
                                pool.wait_ge(s["probs_used"], u * NS)
                            stage_v(u + 1, (r + 1) % 2)
                        if isinstance(u, int):
                            for i in share_of(TRANSFERS, r, d):
                                scatter(i) if u < G else gather(i)

            def before_last():
                for r in range(4):
                    pool.wait_ge(y_stored[r], 16 * TILES // 4)

            pool.wait_ge(s["v_copied"], B)
            stage_v(0, 0)
            pool.wait_ge(s["slots_zeroed"], 16)
            pool.wait_ge(s["routed"], 1)
            pool.wait_ge(s["xn_kept"], 16 * B)
            all_units(pool, unit, None, before_last)

        @block.scalar
        def _(act):
            def roots(begin, end):
                act.wait_ge(s["ln_stats"], end)
                t = slice(begin * T, end * T)
                nc.scalar.activation(std[:, t], mean_var[:, t, 1], ACT.Sqrt, bias=eps_s[:]).then_inc(s["ln_std"], 1)

            def turned(b):
                act.wait_ge(s["xnT_made"], b + 1)
                if past(b):
                    act.wait_ge(s["v_made"], b)
                nc.scalar.copy(xnT[:], pair[0]).then_inc(s["xnT_ready"], 1)

            def sequence(b):
                act.wait_ge(s["logits_made"], b + 1)
                nc.scalar.copy(logits[:, bass.ds(b * T, T), :],
                               pair[2][:, 0:T * E].rearrange("p (t e) -> p t e", e=E)).then_inc(s["logits_copied"], 1)
                act.wait_ge(s["v_made"], b + 1)
                nc.scalar.copy(v_all[:, bass.ds(b * G, G), :, :].rearrange("p g t e -> p t g e"),
                               pair[1].rearrange("p (t g e) -> p t g e", t=T, g=G)).then_inc(s["v_copied"], 1)
                if more_sequences(b):
                    turned(b + 1)
                else:
                    act.wait_ge(s["rt_shifted"], 1)
                    nc.scalar.activation(rt[1], rt[0], ACT.Exp).then_inc(s["rt_exped"], 1)
                if past(b):
                    act.wait_ge(parts_written[0], 16 * PARTS * b)
                act.wait_ge(s["roped"], 2 * b + 1)
                nc.scalar.copy(qsplit[:, 0, :], qr).then_inc(s["q_first"], 1)
                act.wait_ge(s["q_rest"], b + 1)
                nc.scalar.copy(qsplit[:, 1, :], qr).then_inc(s["q_first"], 1)
                if past(b):
                    act.wait_ge(parts_written[1], 16 * PARTS * b)
                act.wait_ge(s["roped"], 2 * b + 2)
                nc.scalar.copy(ksplit[:, 0, :], kr).then_inc(s["k_first"], 1)
                act.wait_ge(s["k_rest"], b + 1)
                nc.scalar.copy(ksplit[:, 1, :], kr).then_inc(s["k_first"], 1)

            act.wait_ge(s["eps_ready"], 1)
            nc.scalar.activation(table_s[:, 0:1], eps_s[:], ACT.Sqrt).then_inc(s["table_loaded"], 1)
            roots(0, 1)
            roots(1, 2)
            turned(0)
            roots(2, B)
            nc.scalar.activation(table_s[:, 1:2], eps_s[:], ACT.Exp).then_inc(s["table_loaded"], 1)
            sequence(0)
            with act.Fori(1, B - 1) as b:
                sequence(b)
            sequence(B - 1)

            def unit(u, begin=0, end=NS):
                for n in range(begin, end):
                    c, kb, q0 = STEPS[n]
                    if n >= 3 or past(u):
                        act.wait_ge(s["probs_used"], u * NS + n - 2)
                    for h in range(HG):
                        at = n * HG + h
                        act.wait_ge(s["scoresT_made"], u * (NS * HG) + at + 1)
                        nc.scalar.activation(probs[n % 3][:, h, q0:HALF], st_of(at)[:, 0:HALF - q0], ACT.Exp,
                                             scale=SCALE).then_inc(s["probs_made"], 1)

            def tile_T(j, r):
                act.wait_ge(s["xT_made"], j + 1)
                nc.scalar.copy(xtT[r % 2], ms[r % 2][:, 2 * P:3 * P]).then_inc(s["xT_ready"], 1)

            def stage_w1(j, r):
                e = act.value_load(expert[0:1, bass.ds(j, 1)], min_val=0, max_val=E - 1)
                if not isinstance(j, int) or j >= 2:
                    act.wait_ge(s["h_made"], 2 * (j - 1))
                    act.wait_ge(s["hid_low"], 2 * (j - 1))
                    act.wait_ge(s["hid_high"], 2 * (j - 1))
                    act.sem_inc(s["w1_free"], 1)
                nc.scalar.copy(w_s[r % 2][:, 0:F + FC], early[:, bass.ds(e * WIDE, F + FC)]).then_inc(s["w1_staged"], 1)

            def tile(j, r):
                if not isinstance(j, int) or j + 1 < TILES:
                    stage_w1(j + 1, r + 1)
                if past(j) and not (isinstance(j, int) and j < 2):
                    act.wait_ge(s["y_made"], j - 1)
                act.wait_ge(s["h_made"], 2 * j + 1)
                act.wait_ge(s["w1_staged"], j + 1)
                for f in range(FC // 2):
                    nc.scalar.activation(hid[r % 2][:, f * P:(f + 1) * P], ms[r % 2][:, f * P:(f + 1) * P], ACT.Relu,
                                         bias=w_s[r % 2][:, F + f:F + f + 1]).then_inc(s["hid_low"], 1)
                if not isinstance(j, int) or j + 1 < TILES:
                    tile_T(j + 1, r + 1)

            def experts():
                act.wait_ge(s["experts_loaded"], 16)
                stage_w1(0, 0)
                tile_T(0, 0)
                all_tiles(act, tile)

            act.wait_ge(s["slots_zeroed"], 16)
            unit(0)
            with act.Fori(1, LAST) as u:
                unit(u)
            unit(LAST, 0, LEAD)
            experts()
            unit(LAST, LEAD)
            with act.Fori(LAST + 1, UNITS) as u:
                unit(u)

        @block.vector
        def _(dve):
            v = nc.vector

            def row_stats(b):
                dve.wait_ge(x_loaded[b], 16)
                for t in range(b * T, (b + 1) * T):
                    last = v.bn_stats(halves[:, t, :], x_all[:, t, :])
                last.then_inc(s["ln_halves"], 1)
                dve.wait_ge(s["ln_halves"], b + 1)
                for t in range(b * T, (b + 1) * T):
                    last = v.bn_aggr(mean_var[:, t, :], halves[:, t, :])
                last.then_inc(s["ln_stats"], 1)

            def normalise(b):
                dve.wait_ge(s["ln_std"], b + 1 if isinstance(b, int) and b == 0 else 3)
                cols = bass.ds(b * T, T)
                v.reciprocal(rstd[:, cols], std[:, cols]).then_inc(s["ln_rstd"], 1)
                dve.wait_ge(s["ln_rstd"], b + 1)
                if past(b):
                    dve.wait_ge(s["xnT_made"], b)
                    dve.wait_ge(s["xn_kept"], 16 * b)
                for t in range(T):
                    col = bass.ds(b * T + t, 1)
                    last = v.tensor_scalar(xn[:, t, :],
                                           x_all[:, col, :].rearrange("p o c -> p (o c)"),
                                           mean_var[:, col, 0], rstd[:, col], ALU.subtract, ALU.mult)
                last.then_inc(s["xn_ready"], 1)

            def cosine(b, made, used, ps, t, n):
                dve.wait_ge(s[made], b + 1)
                if past(b):
                    dve.wait_ge(s["roped"], 2 * b + n - 2)
                v.tensor_tensor(t, ps, cos_s, ALU.mult).then_inc(s[used], 1)

            def sine(b, made, used, split, ps, r):
                dve.wait_ge(s[made], b + 1)
                if past(b):
                    dve.wait_ge(s[split], b)
                v.tensor_tensor(r, ps, sin_s, ALU.mult).then_inc(s[used], 1)

            def third(b, first, rest, split, r, parts):
                dve.wait_ge(s[first], 2 * b + 2)
                dve.wait_ge(s[rest], b + 1)
                v.tensor_tensor(parts[:, 2, :], r, parts[:, 1, :], ALU.subtract).then_inc(s[split], 1)

            def third_q(b):
                third(b, "q_first", "q_rest", "q_split", qr, qsplit)

            def third_k(b):
                third(b, "k_first", "k_rest", "k_split", kr, ksplit)

            def sequence(b):
                cosine(b, "q_made", "q_used", pair[1], tq, 1)
                if more_sequences(b):
                    normalise(b + 1)
                if past(b):
                    third_q(b - 1)
                sine(b, "qs_made", "qs_used", "q_split", pair[2], qr)
                cosine(b, "k_made", "k_used", pair[3], tk, 2)
                if past(b):
                    third_k(b - 1)
                sine(b, "ks_made", "ks_used", "k_split", pair[0], kr)

            row_stats(0)
            normalise(0)
            row_stats(1)
            row_stats(2)
            row_stats(3)
            dve.wait_ge(s["tab_loaded"], 16 * 2)
            sequence(0)
            with dve.Fori(1, B - 1) as b:
                sequence(b)
            sequence(B - 1)

            k = Steps(dve, s["rt_step"])

            def wide(t):
                return t.unsqueeze(2).broadcast_to([P, NT, E])

            def step(ins):
                k.done(ins)
                k.settle()

            em = em8.unsqueeze(1).broadcast_to([P, NT, E])
            m0, m1, one1, one2 = rt
            dve.wait_ge(s["logits_copied"], B)
            dve.wait_ge(s["const_loaded"], 16)
            dve.wait_ge(s["xn_ready"], B)
            step(v.reduce_max(r_s[:, 0, :], logits[:], AX_X))
            v.tensor_tensor(m0, logits[:], wide(r_s[:, 0, :]), ALU.subtract).then_inc(s["rt_shifted"], 1)
            dve.wait_ge(s["rt_exped"], 1)
            step(v.reduce_sum(r_s[:, 1, :], m1, AX_X))
            step(v.reciprocal(r_s[:, 0, :], r_s[:, 1, :]))
            step(v.tensor_tensor(m1, m1, wide(r_s[:, 0, :]), ALU.mult))
            for n, one in enumerate((one1, one2)):
                step(v.reduce_max(share[:, n, :], m1, AX_X))
                step(v.tensor_tensor(m0, m1, wide(share[:, n, :]), ALU.is_equal))
                step(v.tensor_tensor(m0, m0, em, ALU.mult))
                step(v.tensor_reduce(r_s[:, 1, :], m0, AX_X, ALU.min))
                step(v.tensor_tensor(one, em, wide(r_s[:, 1, :]), ALU.is_equal))
                if n == 0:
                    step(v.scalar_tensor_tensor(m1, one, -2.0, m1, ALU.mult, ALU.add))
            flat = "p t e -> p (t e)"
            v.tensor_tensor(chosen_b, one1.rearrange(flat), one2.rearrange(flat), ALU.add
                            ).then_inc(s["chosen_ready"], 1)
            step(v.scalar_tensor_tensor(r_s[:, 0, :], share[:, 0, :], 1e-9, share[:, 1, :], ALU.add, ALU.add))
            step(v.reciprocal(r_s[:, 1, :], r_s[:, 0, :]))
            step(v.tensor_tensor(share[:], share[:], r_s[:, 1, :].unsqueeze(1).broadcast_to([P, 2, NT]), ALU.mult))
            step(v.tensor_tensor(gates[:], one1, wide(share[:, 0, :]), ALU.mult))
            step(v.tensor_tensor(m1, one2, wide(share[:, 1, :]), ALU.mult))
            v.tensor_tensor(gates[:], gates[:], m1, ALU.add).then_inc(s["chosen_ready"], 1)

            third_q(B - 1)
            third_k(B - 1)
            dve.wait_ge(s["consts_ready"], 1)
            def read_item(u, r, n):
                qb, hs, step = ITEMS[n]
                w = (qb + 1) * P
                at = ms[(r * MI + n) % 2]
                dve.wait_ge(s["scores_made"], u * MI + n + 1)
                src = at[:, 0:w] if len(hs) == 1 else at[:, 0:len(hs) * step].rearrange(
                    "p (h w) -> p h w", w=step)[:, :, 0:w]
                v.reduce_max(mx[r % 2][:, hs[0]:hs[-1] + 1, qb], src, AX_X).then_inc(s["scores_read"], 1)

            def split_max(u, r):
                dve.wait_ge(s["scores_read"], u * MI + NI)
                m = mx[r % 2][:].rearrange("p h t -> p (h t)")
                w = HG * T
                neg = mneg[r % 2]
                v.tensor_scalar(neg[:, 0:w], m, -1.0, None, ALU.mult).then_inc(s["mneg_ready"], 1)
                dve.wait_ge(s["mneg_ready"], 2 * u + 1)
                v.scalar_tensor_tensor(neg[:, w:2 * w], m, -1.0, neg[:, 0:w], ALU.mult, ALU.subtract
                                       ).then_inc(s["mneg_ready"], 1)

            def copy_rows(u, r):
                dve.wait_ge(s["scores_made"], u * MI + MI)
                dve.wait_ge(s["mneg_ready"], 2 * u + 2)
                if not isinstance(u, int) or u >= 2:
                    dve.wait_ge(mrow_stored[r % 2], 16 * u if r % 2 == 0 else 16 * (u - 1))
                src = ms[(r * MI + NI) % 2][0:2 * HG * T, 0:P // 2].bitcast(BF16)
                v.tensor_copy(mrow[r % 2][:], src).then_inc(s["scores_read"], 1)

            def heads_out(u, c):
                dve.wait_ge(s["probs_used"], u * NS + (4, NS)[c])
                if past(u):
                    dve.wait_ge(heads_stored[c], 64 * u)
                v.tensor_copy(oraw[c], pv).then_inc(s["heads_copied"], 1)

            def unit(u, r):
                for j in range(NS):
                    for ahead, n in plan_of(u, j):
                        if more(u, ahead):
                            read_item(u + ahead, (r + ahead) % 4, n)
                    if j == TURN - 1 and more(u, 1):
                        split_max(u + 1, (r + 1) % 4)
                    if j == TURN and more(u, 1):
                        copy_rows(u + 1, (r + 1) % 4)
                    if j == 3:
                        heads_out(u, 0)
                    if j == NS - 1:
                        heads_out(u, 1)
                    if isinstance(u, int) and u == UNITS - 1 and j == 6:
                        invert_sums(B - 1)
                    if isinstance(u, int) and u >= LAST:
                        for n in share_of(COMBINES, r, j):
                            combine(n)
                        if u == LAST + 1 and j in INVERTS:
                            invert_sums(INVERTS[j])
                        if (u, j) in FINISHES:
                            finish_heads(FINISHES[u, j])
                        if (u, j - 1) in PROJECTS:
                            add_projection(PROJECTS[u, j - 1])

            def combine(n):
                t, k2 = gather_order(n)
                dve.wait_ge(gathered[n % GOT], 16 * (n // GOT + 1))
                dve.wait_ge(s["acc_loaded"], 16)
                if n >= 2:
                    dve.wait_ge(s["combined"], n - 1)
                v.scalar_tensor_tensor(acc[:, t, :], got[n % GOT], share[:, k2, t:t + 1], acc[:, t, :], ALU.mult,
                                       ALU.add).then_inc(s["combined"], 1)

            def invert_sums(b):
                dve.wait_ge(s["sums_loaded"], 16 * (B + 1) if b == B - 1 else 16 * (B - 1))
                rows = slice(0, (2 * H - HG) * CK if b == B - 1 else P)
                v.reciprocal(sums_s[rows, b, :], sums_s[rows, b, :]).then_inc(s["sums_inverted"], 1)

            def finish_heads(b):
                dve.wait_ge(late_loaded[b], 32)
                v.tensor_tensor(heads_s[b], heads_s[b], over_s[b], ALU.mult).then_inc(s["att_ready"], 1)

            def add_projection(b):
                dve.wait_ge(s["proj_made"], b + 1)
                dve.wait_ge(s["combined"], 2 * T * (b + 1))
                a = acc[:, b * T:(b + 1) * T, :].rearrange("p t c -> p (t c)")
                v.tensor_tensor(a, ms[(UNITS * MI + b) % 2], a, ALU.add).then_inc(s["scores_read"], 1)

            def expert_of(j):
                return dve.value_load(expert[0:1, bass.ds(j, 1)], min_val=0, max_val=E - 1)

            def stage_w2(j, r, e):
                if not isinstance(j, int) or j >= 2:
                    dve.wait_ge(s["y_made"], j - 1)
                    dve.sem_inc(s["w2_free"], 1)
                v.tensor_copy(w_s[r % 2][:, F + FC:WIDE], early[:, bass.ds(e * WIDE + (F + FC), F)]
                              ).then_inc(s["w2_staged"], 1)

            def copy_y(j, r):
                dve.wait_ge(s["y_made"], j + 1)
                if not isinstance(j, int) or j >= 4:
                    dve.wait_ge(y_stored[r % 4], 4 * (j - r % 4))
                v.tensor_copy(yst[r % 4], pv[:, 0:C]).then_inc(s["y_copied"], 1)

            def tile(j, r):
                if not isinstance(j, int) or j >= 2:
                    dve.wait_ge(s["y_made"], j - 1)
                dve.wait_ge(s["h_made"], 2 * j + 2)
                dve.wait_ge(s["w1_staged"], j + 1)
                for f in range(FC // 2, FC):
                    v.tensor_scalar(hid[r % 2][:, f * P:(f + 1) * P],
                                    ms[r % 2][:, HALF + (f - 2) * P:HALF + (f - 1) * P],
                                    w_s[r % 2][:, F + f:F + f + 1], 0.0, ALU.add, ALU.max).then_inc(s["hid_high"], 1)
                following = not isinstance(j, int) or j + 1 < TILES
                if following:
                    e = expert_of(j + 1)
                if past(j):
                    copy_y(j - 1, (r - 1) % 4)
                if following:
                    stage_w2(j + 1, r + 1, e)

            def experts():
                dve.wait_ge(s["experts_loaded"], 16)
                stage_w2(0, 0, expert_of(0))
                all_tiles(dve, tile)
                copy_y(TILES - 1, (TILES - 1) % 4)

            for n in range(NI):
                read_item(0, 0, n)
            split_max(0, 0)
            copy_rows(0, 0)
            total, upto, place, _ = rt2
            et = "p (e t) -> p e t"
            earlier = bank[:, 0, 0:NT * E].rearrange("p (t e) -> p t e", e=E)
            inblock = bank[:, 0, NT * E:2 * NT * E].rearrange("p (t e) -> p e t", e=E)
            dve.wait_ge(s["counted"], 1)
            step(v.tensor_copy(total.rearrange(et, e=E), inblock))
            step(v.tensor_tensor_scan(upto, inner, total, 0.0, ALU.mult, ALU.add))
            count = upto.rearrange(et, e=E)[:, :, NT - 1:NT].rearrange("p e o -> p (e o)")
            step(v.tensor_scalar(r_i[:, 0, :], count, float(ROUND - 1), None, ALU.add))
            bits = ROUND.bit_length() - 1
            step(v.tensor_scalar(r_i[:, 1, :], r_i[:, 0, :], bits, bits, ALU.logical_shift_right,
                                 ALU.logical_shift_left))
            step(v.tensor_copy(r_e[:, 0, :], r_i[:, 1, :]))
            step(v.memset(r_e[:, 3, :], 1.0))
            step(v.tensor_tensor_scan(r_e[:, 1, :], r_e[:, 3, :], r_e[:, 0, :], 0.0, ALU.mult, ALU.add))
            step(v.tensor_tensor(r_e[:, 2, :], r_e[:, 1, :], r_e[:, 0, :], ALU.subtract))
            step(v.tensor_tensor(upto, upto, total, ALU.subtract))
            step(v.tensor_tensor(upto.rearrange(et, e=E), upto.rearrange(et, e=E),
                                 r_e[:, 2, :].unsqueeze(2).broadcast_to([P, E, NT]), ALU.add))
            place = place.rearrange("p (t e) -> p t e", e=E)
            step(v.tensor_tensor(place, earlier, upto.rearrange("p (e t) -> p t e", e=E), ALU.add))
            for n, one in enumerate((one1, one2)):
                step(v.tensor_tensor(m0, one, place, ALU.mult))
                step(v.reduce_sum(r_s[:, n, :], m0, AX_X))
                step(v.tensor_copy(slot[:, n, :], r_s[:, n, :]))
            dve.wait_ge(s["v_made"], B)
            step(v.tensor_tensor(below, r_e[:, 1, :].unsqueeze(1).broadcast_to([P, TILES, E]),
                                 starts.unsqueeze(2).broadcast_to([P, TILES, E]), ALU.is_le))
            step(v.reduce_sum(ends, below, AX_X))
            step(v.tensor_scalar(expert[:], ends, float(E - 1), None, ALU.min))
            dve.wait_ge(s["gT_made"], 1)
            dve.wait_ge(s["xn_kept"], 16 * B)
            v.tensor_copy(gT.rearrange("p a b -> p (a b)"), bank[:, 1, 0:2 * P]).then_inc(s["routed"], 1)

            for n in range(AT_START):
                read_item(1, 1, n)
            all_units(dve, unit, None, experts)
            for c, n in ((0, H), (1, H - HG)):
                dve.wait_ge(last_loaded[c], 32)
                at = slice(0, n * DH), slice(c * HALF, (c + 1) * HALF)
                v.tensor_tensor(heads_s[B - 1][at], heads_s[B - 1][at], over_s[B - 1][at], ALU.mult
                                ).then_inc(s["att_ready"], 1)
            dve.wait_ge(s["sums_spread"], 1)
            v.reciprocal(over_last, st[0]).then_inc(s["over_made"], 1)
            dve.wait_ge(s["over_made"], 1)
            v.tensor_tensor(heads_last, oraw[1], over_last, ALU.mult).then_inc(s["att_ready"], 1)
            for c in range(2):
                dve.wait_ge(s["proj_made"], B + c)
                dve.wait_ge(s["combined"], 2 * NT)
                t0 = (B - 1) * T + c * CK
                a = acc[:, t0:t0 + CK, :].rearrange("p t c -> p (t c)")
                at = ms[(UNITS * MI + B - 1) % 2][:, c * HALF:(c + 1) * HALF]
                v.tensor_tensor(a, at, a, ALU.add).then_inc(s["scores_read"], 1)

        @block.tensor
        def _(pe):
            mm = nc.tensor.matmul
            pe.wait_ge(s["const_loaded"], 16)
            pe.wait_ge(s["w_loaded"], 16 * 2)

            def sequence(b):
                pe.wait_ge(s["xn_ready"], b + 1)
                if past(b):
                    pe.wait_ge(s["ks_used"], b)
                for t in range(T):
                    last = nc.tensor.transpose(pair[0][:, t * P:(t + 1) * P], xn[:, t, :], ident)
                last.then_inc(s["xnT_made"], 1)
                pe.wait_ge(s["xnT_ready"], b + 1)
                for w, ps, made, free in ((0, 1, "q_made", "v_copied"), (1, 2, "qs_made", "logits_copied"),
                                          (2, 3, "k_made", "k_used"), (3, 0, "ks_made", None)):
                    if free and past(b):
                        pe.wait_ge(s[free], b)
                    for c in range(2):
                        last = mm(pair[ps][:, c * HALF:(c + 1) * HALF], w_proj[:, w, :],
                                  xnT[:, c * HALF:(c + 1) * HALF], start=True, stop=True)
                    last.then_inc(s[made], 1)
                pe.wait_ge(s["qs_used"], b + 1)
                for t in range(T):
                    last = mm(pair[2][:, t * E:(t + 1) * E], xnT[:, t * P:(t + 1) * P], w_router[:],
                              start=True, stop=True)
                last.then_inc(s["logits_made"], 1)
                pe.wait_ge(s["q_used"], b + 1)
                for t in range(T):
                    last = mm(pair[1][:, t * C:(t + 1) * C], xnT[:, t * P:(t + 1) * P], w_proj[:, 4, :],
                              start=True, stop=True)
                last.then_inc(s["v_made"], 1)

            sequence(0)
            with pe.Fori(1, B) as b:
                sequence(b)

            pe.wait_ge(s["ks_used"], B)
            pe.wait_ge(s["consts_ready"], 1)
            pe.wait_ge(s["chosen_ready"], 1)
            mm(bank[:, 0, 0:NT * E], before_b[:], chosen_b, start=True, stop=True)
            mm(bank[:, 0, NT * E:2 * NT * E], ones_b[:], chosen_b, start=True, stop=True).then_inc(s["counted"], 1)
            pe.wait_ge(s["chosen_ready"], 2)
            for a in range(2):
                last = nc.tensor.transpose(bank[:, 1, a * P:(a + 1) * P],
                                           gates[:, a * NT // 2:(a + 1) * NT // 2, :].rearrange("p t e -> p (t e)"),
                                           ident)
            last.then_inc(s["gT_made"], 1)

            def score_item(u, r, n):
                qb, hs, step = ITEMS[n]
                w = (qb + 1) * P
                at = ms[(r * MI + n) % 2]
                if not (isinstance(u, int) and u * MI + n < 2):
                    pe.wait_ge(s["scores_read"], u * MI + n - 1)
                for i, h in enumerate(hs):
                    lhsT = qstk[r][0:KROWS, h, qb * P:(qb + 1) * P]
                    for k0 in range(0, w, HALF):
                        k1 = min(w, k0 + HALF)
                        mm(at[:, i * step + k0:i * step + k1], lhsT, kstk[r][0:KROWS, h, k0:k1],
                           start=True, stop=k1 < w)
                    last = mm(at[:, i * step + qb * P:i * step + w], ident_b[:], mask_b[:], start=False, stop=True)
                last.then_inc(s["scores_made"], 1)

            def turn_max(u, r):
                pe.wait_ge(s["mneg_ready"], 2 * u + 2)
                pe.wait_ge(s["scores_read"], u * MI + NI - 1)
                nc.tensor.transpose(ms[(r * MI + NI) % 2][:, 0:P // 2].bitcast(BF16), mneg[r % 2][:],
                                    ident_b[:]).then_inc(s["scores_made"], 1)

            def score(u, r, n, h):
                c, kb, q0 = STEPS[n]
                at = n * HG + h
                if not (isinstance(u, int) and u * NS * HG + at < 3):
                    pe.wait_ge(s["probs_made"], u * (NS * HG) + at - 2)
                mm(st_of(at)[:, 0:HALF - q0], kstk[r][:, h, kb * P:(kb + 1) * P],
                   qstk[r][:, h, c * HALF + q0:(c + 1) * HALF], start=True, stop=True
                   ).then_inc(s["scoresT_made"], 1)

            def products(u, r, n):
                c, kb, q0 = STEPS[n]
                if n == 0:
                    pe.wait_ge(s["v_staged"], u + 1)
                if kb == 0 and (c or past(u)):
                    pe.wait_ge(s["heads_copied"], 2 * u + c)
                pe.wait_ge(s["probs_made"], u * (NS * HG) + (n + 1) * HG)
                if kb >= 4 * c:
                    pe.wait_ge(s["diag_masked"], u * 8 + c * 4 + (kb - 4 * c) + 1)
                for h in range(HG):
                    last = mm(pv[32 * h:32 * h + 32, q0:HALF], vst[r % 2][:, kb, h, :], probs[n % 3][:, h, q0:HALF],
                              start=kb == 0, stop=kb == 4 * c + 3)
                last.then_inc(s["probs_used"], 1)

            def unit(u, r):
                for j in range(NS):
                    ahead, n = divmod(j + LEAD, NS)
                    todo = [(u + a, (r + a) % 4, m) for a, m in plan_of(u, j) if more(u, a)]
                    if ahead and n == 0 and more(u, 1):
                        pe.wait_ge(mrow_stored[(r + 1) % 2], mrow_count(u + 1, r + 1))
                    if j == FIRST and more(u, 2):
                        pe.wait_ge(stack_loaded[(r + 2) % 4], stack_count(u + 2, (r + 2) % 4))
                    for h in range(HG):
                        if more(u, ahead):
                            score(u + ahead, (r + ahead) % 4, n, h)
                        if h and todo:
                            score_item(*todo.pop(0))
                    for item in todo:
                        score_item(*item)
                    if j == TURN and more(u, 1):
                        turn_max(u + 1, (r + 1) % 4)
                    products(u, r, j)
                    if isinstance(u, int) and (u, j) in PROJECTS:
                        project(PROJECTS[u, j])

            LOADS = 3 * PARTS - 1

            def mrow_count(u, r):
                return 16 * (u + 2 - r % 2)

            def stack_count(u, r):
                return (16 * LOADS // 4) * (u - r + 4)

            def hidden(j, r):
                at = ms[r % 2]
                pe.wait_ge(s["xT_ready"], j + 1)
                pe.wait_ge(s["w1_staged"], j + 1)
                for f in range(FC):
                    col = f * P if f < 2 else HALF + (f - 2) * P
                    last = mm(at[:, col:col + P], w_s[r % 2][:, f * P:(f + 1) * P], xtT[r % 2],
                              start=True, stop=True)
                    if f % 2:
                        last.then_inc(s["h_made"], 1)

            def turn_tile(j, r):
                pe.wait_ge(xt_loaded[r % 4], 4 * (j - r % 4) + 16)
                if past(j) and not (isinstance(j, int) and j < 2):
                    pe.wait_ge(s["hid_low"], 2 * (j - 1))
                nc.tensor.transpose(ms[r % 2][:, 2 * P:3 * P], xt[r % 4], ident).then_inc(s["xT_made"], 1)

            def results(j, r):
                pe.wait_ge(s["hid_low"], 2 * (j + 1))
                pe.wait_ge(s["hid_high"], 2 * (j + 1))
                pe.wait_ge(s["w2_staged"], j + 1)
                if past(j):
                    pe.wait_ge(s["y_copied"], j)
                for f in range(FC):
                    last = mm(pv[:, 0:C], hid[r % 2][:, f * P:(f + 1) * P],
                              w_s[r % 2][:, F + FC + f * C:F + FC + (f + 1) * C], start=f == 0, stop=f == FC - 1)
                last.then_inc(s["y_made"], 1)

            def tile(j, r):
                hidden(j, r)
                if not isinstance(j, int) or j + 1 < TILES:
                    turn_tile(j + 1, (r + 1) % 4)
                if past(j):
                    results(j - 1, (r - 1) % 4)

            def experts():
                pe.wait_ge(s["scores_read"], HALFWAY)
                pe.wait_ge(s["heads_copied"], 2 * LAST)
                turn_tile(0, 0)
                all_tiles(pe, tile)
                results(TILES - 1, (TILES - 1) % 4)
                pe.wait_ge(s["y_copied"], TILES)

            def bias_rows(ps, b, c):
                bt = (b % 2) * T + c * CK
                mm(ps, gT[:, b // 2, :], b2_blk[:, bt:bt + CK, :].rearrange("p t c -> p (t c)"),
                   start=True, stop=False)

            def project(b):
                at = ms[(UNITS * MI + b) % 2]
                pe.wait_ge(s["att_ready"], b + 1)
                pe.wait_ge(s["scores_read"], UNITS * MI + b - 1)
                pe.wait_ge(s["b2_loaded"], 16 * (NT // 2))
                for c in range(2):
                    ps = at[:, c * HALF:(c + 1) * HALF]
                    bias_rows(ps, b, c)
                    for t in range(CK):
                        col = (c * CK + t) * P
                        last = mm(ps[:, t * C:(t + 1) * C], heads_s[b][:, col:col + P],
                                  w_proj[:, 5, :], start=False, stop=t == CK - 1)
                last.then_inc(s["proj_made"], 1)

            pe.wait_ge(s["v_copied"], B)
            pe.wait_ge(s["logits_copied"], B)
            pe.wait_ge(s["k_used"], B)
            pe.wait_ge(s["ks_used"], B)
            pe.wait_ge(s["consts_ready"], 1)
            pe.wait_ge(stack_loaded[0], stack_count(0, 0))
            for n in range(NI):
                score_item(0, 0, n)
            turn_max(0, 0)
            pe.wait_ge(stack_loaded[1], stack_count(1, 1))
            for n in range(AT_START):
                score_item(1, 1, n)
            pe.wait_ge(mrow_stored[0], mrow_count(0, 0))
            pe.wait_ge(s["routed"], 1)
            for n in range(LEAD):
                for h in range(HG):
                    score(0, 0, n, h)
            all_units(pe, unit, None, experts)
            pe.wait_ge(s["heads_copied"], 2 * UNITS)
            pe.wait_ge(s["probs_made"], UNITS * NS * HG)
            mm(st[0], sum_rows, oraw[1], start=True, stop=True).then_inc(s["sums_spread"], 1)
            at = ms[(UNITS * MI + B - 1) % 2]
            pe.wait_ge(s["scores_read"], UNITS * MI + B - 2)
            for c, n in ((0, H), (1, H - HG)):
                pe.wait_ge(s["att_ready"], B + c)
                ps = at[:, c * HALF:(c + 1) * HALF]
                bias_rows(ps, B - 1, c)
                for t in range(CK):
                    col = (c * CK + t) * P
                    last = mm(ps[:, t * C:(t + 1) * C], heads_s[B - 1][0:n * DH, col:col + P],
                              w_proj[0:n * DH, 5, :], start=False, stop=c == 0 and t == CK - 1)
                if c == 0:
                    last.then_inc(s["proj_made"], 1)
            pe.wait_ge(s["att_ready"], B + 2)
            for t in range(CK):
                last = mm(ps[:, t * C:(t + 1) * C], heads_last[:, t * P:(t + 1) * P], w_proj[:, 6, :],
                          start=False, stop=t == CK - 1)
            last.then_inc(s["proj_made"], 1)


def kernel(L0_attn_x, L0_attn_Wq, L0_attn_Wk, L0_attn_Wv, L0_attn_Wo, L0_ffn_router_w, L0_ffn_w1, L0_ffn_b1,
           L0_ffn_w2, L0_ffn_b2):
    import numpy as np
    import concourse.bacc as bacc
    from concourse.bass_utils import run_bass_kernel_spmd

    swap = [h * DH + (d + DH // 2) % DH for h in range(H) for d in range(DH)]
    lay = np.ascontiguousarray
    wq, wk, wv, wo = (np.asarray(w) for w in (L0_attn_Wq, L0_attn_Wk, L0_attn_Wv, L0_attn_Wo))
    inv_freq = (1.0 / np.float32(10000.0) ** (np.arange(0, DH, 2, dtype=np.float32) / DH)).astype(np.float32)
    angle = np.outer(np.arange(S, dtype=np.float32), inv_freq).astype(np.float32)
    angle = np.concatenate([angle, angle], axis=1).T
    sign = np.where(np.arange(DH) < DH // 2, -1.0, 1.0)[:, None]
    wo_last = np.zeros((HG, 32, C), np.float32)
    wo_last[:, 0:DH] = wo.T[(H - HG) * DH:].reshape(HG, DH, C)
    wo_last = wo_last.reshape(P, C)
    consts = np.concatenate([
        np.eye(P), np.triu(np.full((P, P), -BIG), k=1), np.triu(np.ones((P, P)), k=1),
        np.arange(P)[:, None] == np.arange(P) // 32 * 32 + DH,
        np.tile(np.arange(E) - E, (P, 1)), np.tile(np.arange(NT) > 0, (P, E)),
        np.tile(np.arange(TILES) * P, (P, 1))], axis=1).astype(np.float32)
    w1 = np.asarray(L0_ffn_w1).transpose(2, 0, 1)
    b1 = np.asarray(L0_ffn_b1).reshape(E, FC, P).transpose(2, 0, 1)
    w2 = np.asarray(L0_ffn_w2).transpose(0, 2, 1).reshape(E, FC, P, C).transpose(2, 0, 1, 3).reshape(P, E, F)
    arrays = {
        "x": lay(np.asarray(L0_attn_x).reshape(B * S, C)),
        "w_projs": lay(np.stack([wq.T, wq[swap].T, wk.T, wk[swap].T, wv.T, wo.T, wo_last], axis=1)),
        "router": lay(np.asarray(L0_ffn_router_w).T),
        "w_experts": lay(np.concatenate([w1, b1, w2], axis=2).reshape(P, E * WIDE)),
        "b2": lay(np.asarray(L0_ffn_b2)),
        "rope_t": np.stack([np.cos(angle), np.sin(angle) * sign]).astype(np.float32),
        "consts": consts,
    }
    nc = bacc.Bacc("TRN2", target_bir_lowering=False, num_devices=1)
    args = [nc.dram_tensor(f"in_{n}", a.shape, mybir.dt.from_np(a.dtype), kind="ExternalInput").ap()
            for n, a in arrays.items()]
    args.append(nc.dram_tensor("out_0", (B * S, C), F32, kind="ExternalOutput").ap())
    args.append(nc.dram_tensor("parts_d", (2, UNITS, HG, PARTS, DH, S), BF16, kind="Internal").ap())
    args.append(nc.dram_tensor("heads_d", (UNITS, HG, DH + 1, S), F32, kind="Internal").ap())
    args.append(nc.dram_tensor("slots_in_d", (TILES * P, C), F32, kind="Internal").ap())
    args.append(nc.dram_tensor("slots_out_d", (TILES * P, C), F32, kind="Internal").ap())
    args.append(nc.dram_tensor("sums_d", (B, H, S), F32, kind="Internal").ap())
    block_program(nc, *args)
    r = run_bass_kernel_spmd(nc, [{f"in_{n}": a for n, a in arrays.items()}], core_ids=[0])
    return r.results[0]["out_0"].reshape(B, S, C)
```
